# Optimizing a Trainium2 kernel written in Bass

```python
import numpy as np
import jax
import jax.numpy as jnp

def _softmax(x, axis=-1):
    return jax.nn.softmax(x, axis=axis)
def _gelu(x):
    return jax.nn.gelu(x, approximate=True)
def _silu(x):
    return jax.nn.silu(x)
def _sigmoid(x):
    return jax.nn.sigmoid(x)
def _layernorm(x, axis=-1, eps=1e-5):
    m = jnp.mean(x, axis=axis, keepdims=True)
    v = jnp.var(x, axis=axis, keepdims=True)
    return (x - m) / jnp.sqrt(v + eps)
def _scatter_add(tgt, idx, src, axis=0):
    return tgt.at[idx].add(src)
def _segment_sum(src, seg, n):
    return jax.ops.segment_sum(src, seg, n)

kernel_name = 'mk_conv_seq_d1_conv_nchw512_70007c'

def setup_inputs(seed: int = 0):
    np.random.seed(seed)
    _w = jnp.asarray
    def _rec_inputs():
        import jax
        import jax.numpy as jnp
        _gk = jax.random.key(seed)
        x = -9.26e-05 + 0.9999 * jax.random.normal(jax.random.fold_in(_gk, 1), (8, 512, 96, 96), jnp.float32)
        return x
    x = _rec_inputs()
    def _L0_conv_setup():
        import jax, jax.numpy as jnp
        import numpy as np
        key = jax.random.key(seed)
        ks = jax.random.split(key, 4)
        B, C, H, W = (8, 512, 96, 96)
        Cq = C // 8
        s = 1.0 / np.sqrt(C)
        return {'x': jax.random.normal(ks[0], (B, C, H, W), jnp.float32), 'Wq': jax.random.normal(ks[1], (Cq, C), jnp.float32) * s, 'bq': jnp.zeros((Cq,), jnp.float32), 'Wk': jax.random.normal(ks[2], (Cq, C), jnp.float32) * s, 'bk': jnp.zeros((Cq,), jnp.float32), 'Wv': jax.random.normal(ks[3], (C, C), jnp.float32) * s, 'bv': jnp.zeros((C,), jnp.float32), 'gamma': jnp.full((1,), 0.1, jnp.float32)}
    _L0_conv_all = _L0_conv_setup()
    _L0_conv_in = {k: v for k, v in _L0_conv_all.items() if k in ('Wq', 'bq', 'Wk', 'bk', 'Wv', 'bv', 'gamma', )}
    del _L0_conv_all

    return {
        "x": x,
        "L0_conv_Wq": _L0_conv_in["Wq"],
        "L0_conv_bq": _L0_conv_in["bq"],
        "L0_conv_Wk": _L0_conv_in["Wk"],
        "L0_conv_bk": _L0_conv_in["bk"],
        "L0_conv_Wv": _L0_conv_in["Wv"],
        "L0_conv_bv": _L0_conv_in["bv"],
        "L0_conv_gamma": _L0_conv_in["gamma"],
    }

def reference(x, L0_conv_Wq, L0_conv_bq, L0_conv_Wk, L0_conv_bk, L0_conv_Wv, L0_conv_bv, L0_conv_gamma):
    import jax
    import jax.numpy as jnp
    def _L0_conv_ref(x, Wq, bq, Wk, bk, Wv, bv, gamma):
        import jax, jax.numpy as jnp
        import numpy as np
        """Criss-Cross Attention (CCNet): attend along the row and column strips only.

            x: [B, C, H, W]; Wq/Wk: [C//8, C]; Wv: [C, C]; gamma: [1].
            """
        B, C, H, W = x.shape
        q = jnp.einsum('bchw,oc->bohw', x, Wq) + bq[None, :, None, None]
        k = jnp.einsum('bchw,oc->bohw', x, Wk) + bk[None, :, None, None]
        v = jnp.einsum('bchw,oc->bohw', x, Wv) + bv[None, :, None, None]
        eH = jnp.einsum('bchw,bcpw->bhwp', q, k)
        diag = jnp.eye(H, dtype=bool)[None, :, None, :]
        eH = jnp.where(diag, -jnp.inf, eH)
        eW = jnp.einsum('bchw,bchp->bhwp', q, k)
        att = jax.nn.softmax(jnp.concatenate([eH, eW], axis=3), axis=3)
        attH, attW = (att[..., :H], att[..., H:])
        outH = jnp.einsum('bcpw,bhwp->bchw', v, attH)
        outW = jnp.einsum('bchp,bhwp->bchw', v, attW)
        return gamma.reshape(()) * (outH + outW) + x

    def _gn(v, G=32, eps=1e-5):
        B_, C_, H_, W_ = v.shape
        g = v.reshape(B_, G, C_ // G, H_, W_)
        m = jnp.mean(g, axis=(2, 3, 4), keepdims=True)
        s = jnp.var(g, axis=(2, 3, 4), keepdims=True)
        return ((g - m) / jnp.sqrt(s + eps)).reshape(v.shape)

    def _ln_c(v, eps=1e-6):
        m = jnp.mean(v, axis=1, keepdims=True)
        s = jnp.var(v, axis=1, keepdims=True)
        return (v - m) / jnp.sqrt(s + eps)

    def _ln_t(v, eps=1e-5):
        m = jnp.mean(v, axis=-1, keepdims=True)
        s = jnp.var(v, axis=-1, keepdims=True)
        return (v - m) / jnp.sqrt(s + eps)

    def _to_tokens(v):
        B_, C_, H_, W_ = v.shape
        return v.reshape(B_, C_, H_ * W_).transpose(0, 2, 1)
    def _from_tokens(t, like):
        B_, C_, H_, W_ = like.shape
        return t.transpose(0, 2, 1).reshape(B_, C_, H_, W_)

    x = _L0_conv_ref(x, L0_conv_Wq, L0_conv_bq, L0_conv_Wk, L0_conv_bk, L0_conv_Wv, L0_conv_bv, L0_conv_gamma)
    return x


_drawn_inputs = setup_inputs


def setup_inputs(seed=0):
    import zlib

    import numpy as np

    out = dict(_drawn_inputs(seed))
    spreads = {'L0_conv_bq': (0.0, 0.377), 'L0_conv_bk': (0.0, 0.8), 'L0_conv_bv': (0.0, 0.8)}
    factors = {}
    for name, (base, spread) in spreads.items():
        noise = np.random.default_rng([zlib.crc32(name.encode()), seed]).standard_normal(out[name].shape)
        drawn = base * np.exp(spread * noise) if base else spread * noise
        out[name] = jnp.asarray(drawn.astype(out[name].dtype))
    for name, factor in factors.items():
        out[name] = (out[name] * factor).astype(out[name].dtype)
    return out
```

```python
from contextlib import ExitStack

import concourse.bass as bass
from concourse import mybir

F32 = mybir.dt.float32
F32R = mybir.dt.float32r
BF16 = mybir.dt.bfloat16
ALU = mybir.AluOpType
ACT = mybir.ActivationFunctionType
AX_X = mybir.AxisListType.X

P = 128
MASKED = -1e38
ROW, COL = 0, 1


def criss_cross_attention(nc, x, wqkT, wvT, bqk, bv, gamma, out):
    B, C, H, W = x.shape
    L = H
    assert H == W and C % P == 0 and L <= P
    HW = H * W
    CT = C // P
    CQ = wqkT.shape[1] // 2
    assert 2 * CQ == P

    BLK = 256
    PT = BLK // P
    NB = HW // BLK
    assert NB % 2 == 0 and HW % BLK == 0

    G = 4
    NG = L // G
    U = 4
    NI = NG // U
    assert NG % U == 0 and G * L * 4 <= 2048

    VS = 2 * G
    VU = 4
    NV = L // VS // VU
    assert L % (VS * VU) == 0
    PH3 = CT * 2 * NV * VU

    x_blk = x.rearrange("b (t c) h w -> b c t (h w)", c=P)
    x_acc = x.rearrange("b (t c) h w -> b t c (h w)", c=P)
    out_acc = out.rearrange("b (t c) h w -> b t c (h w)", c=P)
    vT = nc.dram_tensor("v_pixel_major", [B, HW, C], F32, kind="Internal").ap()
    vT_load = {
        ROW: vT.rearrange("b (h w) (t c) -> b t w h c", w=W, c=P),
        COL: vT.rearrange("b (h w) (t c) -> b t h w c", w=W, c=P),
    }

    base = [(nc.sbuf_base + 63) // 64 * 64]

    def place(name, shape, dt, at=None):
        size = 1
        for n in shape[1:]:
            size *= n
        size *= 2 if dt == BF16 else 4
        where = base[0] if at is None else at
        t = nc.alloc_sbuf_tensor_at(name, shape, dt, offset=where)
        if at is None:
            base[0] += (size + 63) // 64 * 64
        return t, where

    qk_a, qk_a_at = place("qk_a", [P, HW], F32)
    qk_b, qk_b_at = place("qk_b", [P, HW], F32)
    acc = [place("acc0", [P, HW], F32, at=qk_a_at)[0], place("acc1", [P, HW], F32, at=qk_b_at)[0]]
    prob_row, prob_row_at = place("prob_row", [L, L, L], F32)
    prob_col, _ = place("prob_col", [L, L, L], F32)
    prob = {ROW: prob_row, COL: prob_col}
    wqk_raw, _ = place("wqk_raw", [P, CT, P], F32, at=prob_row_at)
    wv_raw, _ = place("wv_raw", [P, CT, C], F32, at=prob_row_at + CT * P * 4)
    wqk_hi, _ = place("wqk_hi", [P, CT, P], F32R)
    wqk_lo, _ = place("wqk_lo", [P, CT, P], F32R)
    wv_hi, _ = place("wv_hi", [P, CT, C], F32R)
    wv_lo, _ = place("wv_lo", [P, CT, C], F32R)
    x_raw = [place(f"x_raw{s}", [P, CT, BLK], F32)[0] for s in range(2)]
    split_at = base[0]
    x_hi = [place(f"x_hi{s}", [P, CT, BLK], F32R)[0] for s in range(2)]
    x_lo = [place(f"x_lo{s}", [P, CT, BLK], F32R)[0] for s in range(2)]
    vout_at = base[0]
    v_out = [place(f"v_out{k}", [P, C], F32)[0] for k in range(2 * PT)]
    v_in = [place(f"v_in{u}", [L, VS, P], F32, at=split_at + u * VS * P * 4)[0] for u in range(VU)]
    assert VU * VS * P * 4 <= vout_at - split_at
    q_grp = [place(f"q_grp{u}", [CQ, G, L], F32, at=vout_at + u * G * L * 4)[0] for u in range(U)]
    e_grp = [place(f"e_grp{u}", [L, G, L], F32, at=vout_at + u * G * L * 4)[0] for u in range(U)]
    assert U * G * L * 4 <= base[0] - vout_at
    nmax = {o: place(f"nmax{o}", [L, L], F32)[0] for o in (ROW, COL)}
    esum = {o: place(f"esum{o}", [L, L], F32)[0] for o in (ROW, COL)}
    factor = {o: place(f"factor{o}", [L, L], F32)[0] for o in (ROW, COL)}
    njoint, _ = place("njoint", [L, L], F32)
    shift, _ = place("shift", [L, 2, L], F32)
    scaled, _ = place("scaled", [L, 2, L], F32)
    factor_rowT, _ = place("factor_rowT", [L, L], F32)
    ident, _ = place("ident", [L, L], F32)
    ident_bf, _ = place("ident_bf", [L, L], BF16)
    diag_bf, _ = place("diag_bf", [L, G, L], BF16)
    bqk_col, _ = place("bqk_col", [P, 1], F32)
    bv_col, _ = place("bv_col", [P, CT], F32)
    gamma_col, _ = place("gamma_col", [P, 1], F32)
    gbv_col, _ = place("gbv_col", [P, CT], F32)
    assert base[0] <= nc.sbuf_usable_end

    with ExitStack() as ctx:
        bank = [ctx.enter_context(nc.psum_tensor(f"bank{k}", [P, 512], F32)) for k in range(8)]

        def sem(name):
            return ctx.enter_context(nc.semaphore(name))

        weights_loaded = sem("weights_loaded")
        consts_set = sem("consts_set")
        ident_zero = sem("ident_zero")
        hi_ready = sem("hi_ready")
        weights_split = sem("weights_split")
        gbv_ready = sem("gbv_ready")
        loops_entered = sem("loops_entered")
        x_loaded = [sem(f"x_loaded{s}") for s in range(2)]
        x_hi_ready = sem("x_hi_ready")
        x_split = sem("x_split")
        qk_mm = sem("qk_mm")
        v_mm = sem("v_mm")
        qk_evac = sem("qk_evac")
        v_evac = sem("v_evac")
        v_stored = [sem(f"v_stored{k}") for k in range(2 * PT)]
        k_shifted = sem("k_shifted")
        q_grp_ready = sem("q_grp_ready")
        s_ready = sem("s_ready")
        nmax_ready = sem("nmax_ready")
        e_ready = sem("e_ready")
        stats_T = sem("stats_T")
        shift_ready = sem("shift_ready")
        shift_exp = sem("shift_exp")
        factors_ready = sem("factors_ready")
        factor_T = sem("factor_T")
        factor_row_ready = sem("factor_row_ready")
        dve_chain = sem("dve_chain")
        e_grp_ready = sem("e_grp_ready")
        pT_ready = sem("pT_ready")
        p_act = sem("p_act")
        p_dve = sem("p_dve")
        acc_loaded = [sem(f"acc_loaded{k}") for k in range(2)]
        v_loaded = [sem(f"v_loaded{u}") for u in range(VU)]
        o_mm = sem("o_mm")
        acc_added = sem("acc_added")
        out_stored = [sem(f"out_stored{k}") for k in range(2)]

        BLOCKS = 2
        VTILES = 2 * PT
        STORES = NV * VU

        strip_bank = [bank[k][0:L, 0:G * L].rearrange("p (g l) -> p g l", g=G) for k in range(8)]
        out_bank = [bank[k][:, 0:G * L].rearrange("p (g l) -> p g l", g=G) for k in range(4)]

        q_strips = {
            ROW: qk_a[0:CQ, :].rearrange("c (h w) -> c h w", w=W),
            COL: qk_a[0:CQ, :].rearrange("c (h w) -> c w h", w=W),
        }
        k_strips = {
            ROW: qk_b[0:CQ, :].rearrange("c (h w) -> c h w", w=W),
            COL: qk_b[0:CQ, :].rearrange("c (h w) -> c w h", w=W),
        }
        acc_strips = [
            {
                ROW: a[:, :].rearrange("c (h w) -> c h w", w=W),
                COL: a[:, :].rearrange("c (h w) -> c w h", w=W),
            }
            for a in acc
        ]

        def before_loop(eng, semaphore, value):
            eng.wait_ge(semaphore, value)
            eng.sem_inc(loops_entered, 1)

        block = ctx.enter_context(nc.Block())

        @block.sync
        def _(sp):
            for k in range(2 * PT):
                sp.sem_inc(v_stored[k], 16)
            sp.dma_start(wqk_raw[:, :, :], wqkT.rearrange("(t c) o -> c t o", c=P)).then_inc(weights_loaded, 16)
            sp.dma_start(wv_raw[:, :, :], wvT.rearrange("(t c) o -> c t o", c=P)).then_inc(weights_loaded, 16)
            sp.dma_start(bqk_col[:, :], bqk.rearrange("(c u) -> c u", u=1)).then_inc(weights_loaded, 16)
            with nc.allow_non_contiguous_dma(reason="a few columns of constants"):
                sp.dma_start(bv_col[:, :], bv.rearrange("(t c) -> c t", c=P)).then_inc(weights_loaded, 16)
                sp.dma_start(gamma_col[:, :], gamma.rearrange("(a u) -> a u", u=1).broadcast_to([P, 1])).then_inc(
                    weights_loaded, 16
                )

            def load_block(b, n, s):
                sp.wait_ge(x_split, b * NB + n + 1)
                sp.dma_start(x_raw[s][:, :, :], x_blk[b, :, :, bass.ds(n * BLK, BLK)]).then_inc(x_loaded[s], 16)

            def store_blocks(b, i):
                for s in range(2):
                    for j in range(PT):
                        k = s * PT + j
                        sp.wait_ge(v_evac, (b * NB + 2 * i) * PT + k + 1 + VTILES)
                        sp.dma_start(vT[b, bass.ds((2 * i + s) * BLK + j * P, P), :], v_out[k][:, :]).then_inc(
                            v_stored[k], 16
                        )
                sp.wait_ge(qk_evac, b * NB + 2 * i + 2 + BLOCKS)
                sp.dma_start(
                    qk_b[0:CQ, bass.ds(2 * i * BLK, 2 * BLK)], qk_a[CQ:P, bass.ds(2 * i * BLK, 2 * BLK)]
                ).then_inc(k_shifted, 16)

            with sp.Fori(0, B) as b:
                for s in range(2):
                    load_block(b, s, s)
                before_loop(sp, out_stored[1], b * (CT // 2 * STORES * 16) + 16)
                with sp.Fori(0, NB // 2 - 1) as i:
                    for s in range(2):
                        load_block(b, 2 * i + 2 + s, s)
                    store_blocks(b, i)
                store_blocks(b, NB // 2 - 1)
                sp.wait_ge(s_ready, (b + 1) * (2 * NG) + U)
                for k in range(2):
                    sp.dma_start(acc[k][:, :], x_acc[b, k, :, :]).then_inc(acc_loaded[k], 16)
                for k in range(2 * PT):
                    before_loop(sp, v_stored[k], (b + 1) * (NB // 2 * 16) + 16)
                with sp.Fori(0, CT // 2) as tp:
                    for par in range(2):
                        for o in (COL, ROW):
                            with sp.Fori(0, NV) as i:
                                n3 = ((b * CT + tp * 2 + par) * 2 + (1 - o)) * NV + i
                                for u in range(VU):
                                    sp.wait_ge(o_mm, (n3 * VU + u) * 2 + 2)
                                    sp.dma_start(
                                        v_in[u][:, :, :],
                                        vT_load[o][b, tp * 2 + par, :, bass.ds((i * VU + u) * VS, VS), :],
                                    ).then_inc(v_loaded[u], 16)
            for k in range(2):
                sp.wait_ge(out_stored[k], B * (CT // 2 * STORES * 16) + 16)

        @block.gpsimd
        def _(pool):
            nc.gpsimd.memset(ident[:, :], 0.0).then_inc(ident_zero, 1)
            nc.gpsimd.memset(diag_bf[:, :, :], 0.0).then_inc(ident_zero, 1)
            pool.wait_ge(ident_zero, 2)
            nc.gpsimd.affine_select(
                out=ident[:, :], in_=ident[:, :], compare_op=ALU.not_equal, fill=1.0, base=0,
                pattern=[[-1, L]], channel_multiplier=1,
            ).then_inc(consts_set, 1)
            nc.gpsimd.affine_select(
                out=diag_bf[:, :, :], in_=diag_bf[:, :, :], compare_op=ALU.not_equal, fill=MASKED, base=0,
                pattern=[[0, G], [-1, L]], channel_multiplier=1,
            ).then_inc(consts_set, 1)
            pool.wait_ge(consts_set, 2)
            nc.gpsimd.tensor_copy(ident_bf[:, :], ident[:, :]).then_inc(consts_set, 1)

            with pool.Fori(0, B) as b:
                pool.wait_ge(qk_evac, (b + 1) * NB + BLOCKS)
                for k in range(2 * PT):
                    before_loop(pool, v_stored[k], (b + 1) * (NB // 2 * 16) + 16)
                for o in (ROW, COL):
                    with pool.Fori(0, NI) as i:
                        for u in range(U):
                            pool.wait_ge(s_ready, (b * 2 + o) * NG + i * U + u + 1)
                            nc.gpsimd.tensor_copy(
                                q_grp[u][:, :, :], q_strips[o][:, bass.ds((i * U + u) * G, G), :]
                            ).then_inc(q_grp_ready, 1)
                before_loop(pool, s_ready, (b + 1) * (2 * NG) + U)
                for o in (COL, ROW):
                    if o == COL:
                        before_loop(pool, factors_ready, b + 1)
                    else:
                        before_loop(pool, factor_row_ready, b + 1)
                    with pool.Fori(0, NI) as i:
                        for u in range(U):
                            pool.wait_ge(pT_ready, (b * 2 + 1 - o) * NG + i * U + u + 1)
                            strips = bass.ds((i * U + u) * G, G)
                            nc.gpsimd.tensor_tensor(
                                e_grp[u][:, :, :], prob[o][:, strips, :],
                                factor[o][:, strips].unsqueeze(2).to_broadcast([L, G, L]), ALU.mult,
                            ).then_inc(e_grp_ready, 1)

        @block.scalar
        def _(act):
            act.sem_inc(v_evac, VTILES)
            act.sem_inc(e_ready, U)
            act.sem_inc(p_act, U // 2)
            for k in range(2):
                act.sem_inc(out_stored[k], 16)
            act.wait_ge(weights_loaded, 5 * 16)
            nc.scalar.copy(wqk_hi[:, :, :], wqk_raw[:, :, :]).then_inc(hi_ready, 1)
            nc.scalar.copy(wv_hi[:, :, :], wv_raw[:, :, :]).then_inc(hi_ready, 1)

            def split_hi(b, n, s, sem_round):
                act.wait_ge(x_loaded[s], sem_round)
                act.wait_ge(qk_mm, b * NB + n + 1)
                nc.scalar.copy(x_hi[s][:, :, :], x_raw[s][:, :, :]).then_inc(x_hi_ready, 1)

            def evac_v(b, i, s):
                for j in range(PT):
                    k = s * PT + j
                    tile = (b * NB + 2 * i) * PT + k
                    act.wait_ge(v_mm, tile + 1)
                    act.wait_ge(v_stored[k], (b * (NB // 2) + i) * 16 + 16)
                    nc.scalar.activation(v_out[k][:, :], bank[k][:, :], ACT.Copy, scale=gamma_col[:, 0:1]).then_inc(
                        v_evac, 1
                    )

            with act.Fori(0, B) as b:
                act.wait_ge(o_mm, b * (2 * PH3) + 2 * VU)
                act.wait_ge(pT_ready, b * (2 * NG) + U)
                half = b * (NB // 2)
                split_hi(b, 0, 0, half * 16 + 16)
                with act.Fori(0, NB // 2 - 1) as i:
                    split_hi(b, 2 * i + 1, 1, (half + i) * 16 + 16)
                    evac_v(b, i, 0)
                    split_hi(b, 2 * i + 2, 0, (half + i) * 16 + 32)
                    evac_v(b, i, 1)
                split_hi(b, NB - 1, 1, (half + NB // 2 - 1) * 16 + 16)
                evac_v(b, NB // 2 - 1, 0)
                evac_v(b, NB // 2 - 1, 1)
                for o in (ROW, COL):
                    with act.Fori(0, NI) as i:
                        for u in range(U):
                            act.wait_ge(nmax_ready, (b * 2 + o) * NG + i * U + u + 1)
                            for g in range(G):
                                strip = (i * U + u) * G + g
                                last = nc.scalar.activation(
                                    prob[o][:, bass.ds(strip, 1), :], strip_bank[u][:, g:g + 1, :], ACT.Exp,
                                    bias=nmax[o][:, bass.ds(strip, 1)], accum_out=esum[o][:, bass.ds(strip, 1)],
                                )
                            last.then_inc(e_ready, 1)
                act.wait_ge(shift_ready, b + 1)
                nc.scalar.activation(scaled[:, :, :], shift[:, :, :], ACT.Exp).then_inc(shift_exp, 1)
                for o in (COL, ROW):
                    with act.Fori(0, NI) as i:
                        for u in range(0, U, 2):
                            act.wait_ge(pT_ready, (b * 2 + 1 - o) * NG + i * U + u + 1 + U)
                            nc.scalar.copy(
                                prob[o][:, bass.ds((i * U + u) * G, G), :], strip_bank[4 + u][:, :, :]
                            ).then_inc(p_act, 1)
                for t in range(CT):
                    k = t % 2
                    with act.Fori(0, NV) as i:
                        n3 = ((b * CT + t) * 2 + 1) * NV + i
                        for u in range(VU):
                            act.wait_ge(acc_added, (n3 * VU + u) * 2 + 2 + 4)
                            px = bass.ds((i * VU + u) * (VS * W), VS * W)
                            act.dma_start(out_acc[b, t, :, px], acc[k][:, px]).then_inc(out_stored[k], 16)
                    if t + 2 < CT:
                        act.wait_ge(out_stored[k], (b * (CT // 2) + t // 2 + 1) * (STORES * 16) + 16)
                        act.dma_start(acc[k][:, :], x_acc[b, t + 2, :, :]).then_inc(acc_loaded[k], 16)

        @block.vector
        def _(dve):
            links = [0]
            LINKS = 5

            dve.sem_inc(x_split, BLOCKS)
            dve.sem_inc(qk_evac, BLOCKS)
            dve.sem_inc(p_dve, U // 2)
            dve.sem_inc(acc_added, 4)
            dve.wait_ge(hi_ready, 1)
            nc.vector.tensor_tensor(
                wqk_lo[:, :, :], wqk_raw[:, :, :], wqk_hi[:, :, :].bitcast(F32), ALU.subtract
            ).then_inc(weights_split, 1)
            dve.wait_ge(hi_ready, 2)
            nc.vector.tensor_tensor(
                wv_lo[:, :, :], wv_raw[:, :, :], wv_hi[:, :, :].bitcast(F32), ALU.subtract
            ).then_inc(weights_split, 1)
            nc.vector.tensor_scalar(gbv_col[:, :], bv_col[:, :], gamma_col[:, 0:1], None, ALU.mult).then_inc(
                gbv_ready, 1
            )

            def split_lo(b, n, s):
                dve.wait_ge(x_hi_ready, b * NB + n + 1)
                nc.vector.tensor_tensor(
                    x_lo[s][:, :, :], x_raw[s][:, :, :], x_hi[s][:, :, :].bitcast(F32), ALU.subtract
                ).then_inc(x_split, 1)

            def evac_qk(b, n, s):
                dve.wait_ge(qk_mm, b * NB + n + 1 + BLOCKS)
                nc.vector.tensor_scalar(
                    qk_a[:, bass.ds(n * BLK, BLK)], bank[4 + s][:, 0:BLK], bqk_col[:, 0:1], None, ALU.add
                ).then_inc(qk_evac, 1)

            with dve.Fori(0, B) as b:
                dve.wait_ge(out_stored[0], b * (CT // 2 * STORES * 16) + 16)
                split_lo(b, 0, 0)
                with dve.Fori(0, NB // 2 - 1) as i:
                    split_lo(b, 2 * i + 1, 1)
                    evac_qk(b, 2 * i, 0)
                    split_lo(b, 2 * i + 2, 0)
                    evac_qk(b, 2 * i + 1, 1)
                split_lo(b, NB - 1, 1)
                evac_qk(b, NB - 2, 0)
                evac_qk(b, NB - 1, 1)
                for o in (ROW, COL):
                    with dve.Fori(0, NI) as i:
                        for u in range(U):
                            dve.wait_ge(s_ready, (b * 2 + o) * NG + i * U + u + 1 + U)
                            nc.vector.tensor_reduce(
                                nmax[o][:, bass.ds((i * U + u) * G, G)], strip_bank[u][:, :, :], AX_X, ALU.max,
                                negate=True,
                            ).then_inc(nmax_ready, 1)
                dve.wait_ge(stats_T, b + 1)
                row_nmax, row_esum = bank[0][0:L, 0:L], bank[1][0:L, 0:L]
                nc.vector.tensor_tensor(njoint[:, :], row_nmax, nmax[COL][:, :], ALU.min).then_inc(dve_chain, 1)
                dve.wait_ge(dve_chain, b * LINKS + 1)
                nc.vector.tensor_tensor(shift[:, ROW, :], njoint[:, :], row_nmax, ALU.subtract)
                nc.vector.tensor_tensor(shift[:, COL, :], njoint[:, :], nmax[COL][:, :], ALU.subtract).then_inc(
                    shift_ready, 1
                )
                dve.wait_ge(shift_exp, b + 1)
                nc.vector.tensor_tensor(shift[:, ROW, :], scaled[:, ROW, :], row_esum, ALU.mult).then_inc(dve_chain, 1)
                nc.vector.tensor_tensor(shift[:, COL, :], scaled[:, COL, :], esum[COL][:, :], ALU.mult).then_inc(
                    dve_chain, 1
                )
                dve.wait_ge(dve_chain, b * LINKS + 3)
                nc.vector.tensor_tensor(njoint[:, :], shift[:, ROW, :], shift[:, COL, :], ALU.add).then_inc(dve_chain, 1)
                dve.wait_ge(dve_chain, b * LINKS + 4)
                nc.vector.reciprocal(shift[:, ROW, :], njoint[:, :]).then_inc(dve_chain, 1)
                dve.wait_ge(dve_chain, b * LINKS + 5)
                nc.vector.tensor_tensor(factor_rowT[:, :], scaled[:, ROW, :], shift[:, ROW, :], ALU.mult)
                nc.vector.tensor_tensor(factor[COL][:, :], scaled[:, COL, :], shift[:, ROW, :], ALU.mult).then_inc(
                    factors_ready, 1
                )
                dve.wait_ge(factor_T, b + 1)
                nc.vector.tensor_copy(factor[ROW][:, :], bank[2][0:L, 0:L]).then_inc(factor_row_ready, 1)
                for o in (COL, ROW):
                    with dve.Fori(0, NI) as i:
                        for u in range(1, U, 2):
                            dve.wait_ge(pT_ready, (b * 2 + 1 - o) * NG + i * U + u + 1 + U)
                            nc.vector.tensor_copy(
                                prob[o][:, bass.ds((i * U + u) * G, G), :], strip_bank[4 + u][:, :, :]
                            ).then_inc(p_dve, 1)
                before_loop(dve, gbv_ready, 1)
                with dve.Fori(0, CT // 2) as tp:
                    for par in range(2):
                        for o in (COL, ROW):
                            first = ((b * CT + tp * 2 + par) * 2 + (1 - o)) * NV
                            with dve.Fori(0, NV) as i:
                                if o == COL:
                                    dve.wait_ge(acc_loaded[par], (b * (CT // 2) + tp + 1) * 16)
                                else:
                                    dve.wait_ge(acc_added, first * (2 * VU) + 4)
                                for u in range(VU):
                                    for half in range(2):
                                        n = ((first + i) * VU + u) * 2 + half
                                        dve.wait_ge(o_mm, n + 1 + 2 * VU)
                                        strips = bass.ds(((i * VU + u) * 2 + half) * G, G)
                                        a = acc_strips[par][o][:, strips, :]
                                        prod = out_bank[(2 * u + half) % 4]
                                        if o == COL:
                                            op = nc.vector.scalar_tensor_tensor(
                                                out=a, in0=prod, scalar=gbv_col[:, bass.ds(tp * 2 + par, 1)], in1=a,
                                                op0=ALU.add, op1=ALU.add,
                                            )
                                        else:
                                            op = nc.vector.tensor_tensor(a, prod, a, ALU.add)
                                        op.then_inc(acc_added, 1)

        @block.tensor
        def _(pe):
            pe.sem_inc(qk_mm, BLOCKS)
            pe.sem_inc(s_ready, U)
            pe.sem_inc(pT_ready, U)
            pe.sem_inc(o_mm, 2 * VU)
            pe.wait_ge(weights_split, 2)
            pe.wait_ge(consts_set, 3)

            def three_products(dst, stationary, moving):
                for t in range(CT):
                    (s_hi, s_lo), (m_hi, m_lo) = stationary(t), moving(t)
                    nc.tensor.matmul(dst, s_hi, m_hi, start=(t == 0), stop=False)
                    nc.tensor.matmul(dst, s_hi, m_lo, start=False, stop=False)
                    last = nc.tensor.matmul(dst, s_lo, m_hi, start=False, stop=(t == CT - 1))
                return last

            with pe.Fori(0, B) as b:
                before_loop(pe, acc_added, b * (2 * PH3) + 4)
                with pe.Fori(0, NB // 2) as i:
                    for s in range(2):
                        n = b * NB + 2 * i + s
                        pe.wait_ge(x_split, n + 1 + BLOCKS)
                        for j in range(PT):
                            k = s * PT + j
                            px = slice(j * P, (j + 1) * P)
                            pe.wait_ge(v_evac, (b * NB + 2 * i) * PT + k + 1)
                            three_products(
                                bank[k][:, :],
                                lambda t: (x_hi[s][:, t, px], x_lo[s][:, t, px]),
                                lambda t: (wv_hi[:, t, :], wv_lo[:, t, :]),
                            ).then_inc(v_mm, 1)
                        pe.wait_ge(qk_evac, n + 1)
                        three_products(
                            bank[4 + s][:, 0:BLK],
                            lambda t: (wqk_hi[:, t, :], wqk_lo[:, t, :]),
                            lambda t: (x_hi[s][:, t, :], x_lo[s][:, t, :]),
                        ).then_inc(qk_mm, 1)
                pe.wait_ge(k_shifted, (b + 1) * (NB // 2 * 16))
                before_loop(pe, v_evac, (b + 1) * (NB * PT) + VTILES)
                for o in (ROW, COL):
                    with pe.Fori(0, NI) as i:
                        for u in range(U):
                            n = (b * 2 + o) * NG + i * U + u
                            pe.wait_ge(q_grp_ready, n + 1)
                            pe.wait_ge(e_ready, n + 1)
                            for g in range(G):
                                last = nc.tensor.matmul(
                                    strip_bank[u][:, g, :], q_grp[u][:, g, :],
                                    k_strips[o][:, bass.ds((i * U + u) * G + g, 1), :],
                                    start=(o == ROW or g == 0), stop=(o == ROW),
                                )
                            if o == COL:
                                last = nc.tensor.matmul(
                                    strip_bank[u], ident_bf[:, :], diag_bf[:, :, :], start=False, stop=True
                                )
                            last.then_inc(s_ready, 1)
                pe.wait_ge(e_ready, (b + 1) * (2 * NG) + U)
                nc.tensor.transpose(bank[0][0:L, 0:L], nmax[ROW][:, :], ident[:, :])
                nc.tensor.transpose(bank[1][0:L, 0:L], esum[ROW][:, :], ident[:, :]).then_inc(stats_T, 1)
                pe.wait_ge(factors_ready, b + 1)
                nc.tensor.transpose(bank[2][0:L, 0:L], factor_rowT[:, :], ident[:, :]).then_inc(factor_T, 1)
                for o in (COL, ROW):
                    with pe.Fori(0, NI) as i:
                        for u in range(U):
                            n = (b * 2 + 1 - o) * NG + i * U + u
                            pe.wait_ge(e_grp_ready, n + 1)
                            done = ((b * 2 + 1 - o) * NI + i) * 2 + u // 2 + 1
                            pe.wait_ge(p_dve if u % 2 else p_act, done)
                            for g in range(G):
                                last = nc.tensor.transpose(
                                    strip_bank[4 + u][:, g, :], e_grp[u][:, g, :], ident[:, :]
                                )
                            last.then_inc(pT_ready, 1)
                pe.wait_ge(p_act, (b + 1) * NG + 2)
                before_loop(pe, p_dve, (b + 1) * NG + 2)
                with pe.Fori(0, CT // 2) as tp:
                    for par in range(2):
                        for o in (COL, ROW):
                            with pe.Fori(0, NV) as i:
                                n3 = ((b * CT + tp * 2 + par) * 2 + (1 - o)) * NV + i
                                for u in range(VU):
                                    pe.wait_ge(v_loaded[u], n3 * 16 + 16)
                                    for half in range(2):
                                        pe.wait_ge(acc_added, (n3 * VU + u) * 2 + half + 1)
                                        dst = out_bank[(2 * u + half) % 4]
                                        for g in range(G):
                                            strip = ((i * VU + u) * 2 + half) * G + g
                                            last = nc.tensor.matmul(
                                                dst[:, g, :], v_in[u][:, half * G + g, :],
                                                prob[o][:, bass.ds(strip, 1), :], start=True, stop=True,
                                            )
                                        last.then_inc(o_mm, 1)


def kernel(x, L0_conv_Wq, L0_conv_bq, L0_conv_Wk, L0_conv_bk, L0_conv_Wv, L0_conv_bv, L0_conv_gamma):
    import numpy as np
    import concourse.bacc as bacc
    from concourse.bass_utils import run_bass_kernel_spmd

    arrays = {
        "x": np.ascontiguousarray(x),
        "wqkT": np.ascontiguousarray(np.concatenate([np.asarray(L0_conv_Wq), np.asarray(L0_conv_Wk)], axis=0).T),
        "wvT": np.ascontiguousarray(np.asarray(L0_conv_Wv).T),
        "bqk": np.concatenate([np.asarray(L0_conv_bq), np.asarray(L0_conv_bk)]),
        "bv": np.ascontiguousarray(L0_conv_bv),
        "gamma": np.ascontiguousarray(L0_conv_gamma),
    }
    nc = bacc.Bacc("TRN2", target_bir_lowering=False, num_devices=1)
    args = [
        nc.dram_tensor(n, a.shape, mybir.dt.from_np(a.dtype), kind="ExternalInput").ap() for n, a in arrays.items()
    ]
    out = nc.dram_tensor("out", arrays["x"].shape, F32, kind="ExternalOutput").ap()
    criss_cross_attention(nc, *args, out)
    return run_bass_kernel_spmd(nc, [arrays], core_ids=[0]).results[0]["out"]
```

```python
from contextlib import ExitStack

import concourse.bass as bass
from concourse import mybir

F32 = mybir.dt.float32
F32R = mybir.dt.float32r
F16 = mybir.dt.float16
BF16 = mybir.dt.bfloat16
I32 = mybir.dt.int32
ALU = mybir.AluOpType
ACT = mybir.ActivationFunctionType
AX_X = mybir.AxisListType.X

RMAX = bass.bass_isa.ReduceOp.max

P = 128
EXPONENT = 0x7F800000
TOP = 2.0 ** 14
TINY = 2.0 ** -40
MASKED = -1e38
ROW, COL = 0, 1


def criss_cross_attention(nc, x, wqkT, wvT, bqk, bv, gamma, out):
    B, C, H, W = x.shape
    L = H
    assert H == W and C % P == 0 and L <= P
    HW = H * W
    CT = C // P
    CQ = wqkT.shape[1] // 2
    assert 2 * CQ == P

    BLK = 256
    PT = BLK // P
    NB = HW // BLK
    assert NB % 2 == 0 and HW % BLK == 0

    G = 4
    NG = L // G
    U = 4
    NI = NG // U
    assert NG % U == 0 and G * L * 4 <= 2048

    VS = 2 * G
    VU = 6
    NV = L // VS // VU
    assert L % (VS * VU) == 0
    PH3 = CT * 2 * NV * VU

    x_blk = x.rearrange("b (t c) h w -> b c t (h w)", c=P)
    x_acc = x.rearrange("b (t c) h w -> b t c (h w)", c=P)
    out_acc = out.rearrange("b (t c) h w -> b t c (h w)", c=P)
    vT = nc.dram_tensor("v_pixel_major", [B, HW, CT * 2 * P], F16, kind="Internal").ap()
    vT_load = {
        ROW: vT.rearrange("b (h w) (t a) -> b t w h a", w=W, t=CT),
        COL: vT.rearrange("b (h w) (t a) -> b t h w a", w=W, t=CT),
    }

    base = [(nc.sbuf_base + 63) // 64 * 64]

    def place(name, shape, dt, at=None):
        size = 1
        for n in shape[1:]:
            size *= n
        size *= 2 if dt in (BF16, F16) else 4
        where = base[0] if at is None else at
        t = nc.alloc_sbuf_tensor_at(name, shape, dt, offset=where)
        if at is None:
            step = 64 if size >= 64 else 32
            base[0] += (size + step - 1) // step * step
        return t, where

    acc0, acc0_at = place("acc0", [P, HW], F32)
    acc1, acc1_at = place("acc1", [P, HW], F32)
    acc = [acc0, acc1]
    q_both, _ = place("q_both", [P, HW], F16, at=acc0_at)
    k_hi, _ = place("k_hi", [P, HW], F16, at=acc0_at + 2 * HW)
    k_lo, _ = place("k_lo", [P, HW], F16, at=acc1_at)
    prob_row, prob_row_at = place("prob_row", [L, L, L], F32)
    prob_col, prob_col_at = place("prob_col", [L, L, L], F32)
    prob = {ROW: prob_row, COL: prob_col}
    parts = {
        o: prob[o][:, :, :].bitcast(F16).rearrange("p s (a q) -> p s a q", a=2) for o in (ROW, COL)
    }
    wqk_raw, _ = place("wqk_raw", [P, CT, P], F32, at=prob_row_at)
    wv_raw, _ = place("wv_raw", [P, CT, C], F32, at=prob_row_at + CT * P * 4)
    wqk_hi, _ = place("wqk_hi", [P, CT, P], F32R)
    wqk_lo, _ = place("wqk_lo", [P, CT, P], F32R)
    wv_hi, _ = place("wv_hi", [P, CT, C], F32R)
    wv_lo, _ = place("wv_lo", [P, CT, C], F32R)
    x_raw = [place(f"x_raw{s}", [P, CT, BLK], F32)[0] for s in range(2)]
    x_hi_at = base[0]
    x_hi = [place(f"x_hi{s}", [P, CT, BLK], F32R)[0] for s in range(2)]
    x_lo_at = [0, 0]
    x_lo = [None, None]
    for s in range(2):
        x_lo[s], x_lo_at[s] = place(f"x_lo{s}", [P, CT, BLK], F32R)
    at = prob_col_at
    v_out, qk_f32, x_next = [], [], []
    for k in range(2 * PT):
        v_out.append(place(f"v_out{k}", [P, CT, 2, P], F16, at=at)[0])
        at += C * 4
    for k in range(2):
        x_next.append(place(f"x_next{k}", [P, CT, BLK], F32, at=at)[0])
        at += CT * BLK * 4
    for k in range(2):
        qk_f32.append(place(f"qk_f32{k}", [P, BLK], F32, at=at)[0])
        at += BLK * 4
    q_low, _ = place("q_low", [CQ, HW], F16, at=at)
    assert at + HW * 2 <= prob_col_at + L * L * 4
    assert VS * 2 * P * 2 == CT * BLK * 4
    v_in = [place(f"v_in{u}", [L, VS, 2, P], F16)[0] for u in range(2)]
    v_in += [place(f"v_in{2 + s}", [L, VS, 2, P], F16, at=x_lo_at[s])[0] for s in range(2)]
    late_at = base[0]
    v_in += [place(f"v_in{u}", [L, VS, 2, P], F16)[0] for u in range(4, VU)]
    e_grp = [place(f"e_grp{u}", [L, G, L], F32, at=late_at + u * G * L * 4)[0] for u in range(U)]
    nmax, factor = {}, {}
    for o in (ROW, COL):
        nmax[o], at = place(f"nmax{o}", [L, L], F32)
        factor[o], _ = place(f"factor{o}", [L, L], F32, at=at)
    esum = {o: place(f"esum{o}", [L, L], F32)[0] for o in (ROW, COL)}
    ident, _ = place("ident", [L, L], F32)
    ident_bf, _ = place("ident_bf", [L, L], BF16)
    diag_bf, _ = place("diag_bf", [L, G, L], BF16)
    assert U * G * L * 4 <= 2 * VS * 2 * P * 2
    at = x_hi_at
    njoint, _ = place("njoint", [L, L], F32, at=at)
    shift, _ = place("shift", [L, 2, L], F32, at=at + L * 4)
    scaled, _ = place("scaled", [L, 2, L], F32, at=at + 3 * L * 4)
    factor_rowT, _ = place("factor_rowT", [L, L], F32, at=at + 5 * L * 4)
    bqk_col, _ = place("bqk_col", [P, 1], F32)
    bv_col, _ = place("bv_col", [P, CT], F32)
    gamma_col, _ = place("gamma_col", [P, 1], F32)
    gbv_col, _ = place("gbv_col", [P, CT], F32)
    wmax_own, _ = place("wmax_own", [P, 3], F32)
    wmax, _ = place("wmax", [P, 3], F32)
    xmax_blk, _ = place("xmax_blk", [P, NB], F32)
    xmax_own, _ = place("xmax_own", [P, 1], F32)
    xmax, _ = place("xmax", [P, 1], F32)
    bound, _ = place("bound", [P, 2], F32)
    floor2, _ = place("floor2", [P, 2], F32)
    unscale, _ = place("unscale", [P, 2], F32)
    SCALE_QK, SCALE_V, BIAS_QK, S_FACTOR, O_FACTOR = range(5)
    scales, _ = place("scales", [P, 5], F32)
    scales_next, _ = place("scales_next", [P, 5], F32)
    assert base[0] <= nc.sbuf_usable_end

    with ExitStack() as ctx:
        bank = [ctx.enter_context(nc.psum_tensor(f"bank{k}", [P, 512], F32)) for k in range(8)]

        def sem(name):
            return ctx.enter_context(nc.semaphore(name))

        weights_loaded = sem("weights_loaded")
        consts_set = sem("consts_set")
        ident_zero = sem("ident_zero")
        hi_ready = sem("hi_ready")
        weights_split = sem("weights_split")
        wmax_own_ready = sem("wmax_own_ready")
        wmax_ready = sem("wmax_ready")
        const_chain = sem("const_chain")
        waits_carried = sem("waits_carried")
        x_next_loaded = [sem(f"x_next_loaded{s}") for s in range(2)]
        x_next_seen = sem("x_next_seen")
        xmax_own_ready = sem("xmax_own_ready")
        xmax_ready = sem("xmax_ready")
        scale_chain = sem("scale_chain")
        x_loaded = [sem(f"x_loaded{s}") for s in range(2)]
        x_hi_ready = sem("x_hi_ready")
        x_split = sem("x_split")
        qk_mm = sem("qk_mm")
        v_mm = sem("v_mm")
        v_hi_ready = sem("v_hi_ready")
        v_ready = sem("v_ready")
        v_stored = [sem(f"v_stored{k}") for k in range(2 * PT)]
        qk_evac = sem("qk_evac")
        qk_hi_ready = sem("qk_hi_ready")
        qk_ready = sem("qk_ready")
        qk_shifted = sem("qk_shifted")
        s_ready = sem("s_ready")
        nmax_raw = sem("nmax_raw")
        nmax_ready = sem("nmax_ready")
        e_ready = sem("e_ready")
        esum_even = sem("esum_even")
        stats_T = sem("stats_T")
        shift_ready = sem("shift_ready")
        shift_exp = sem("shift_exp")
        factors_ready = sem("factors_ready")
        factor_T = sem("factor_T")
        factor_row_ready = sem("factor_row_ready")
        dve_chain = sem("dve_chain")
        e_grp_ready = sem("e_grp_ready")
        pT_ready = sem("pT_ready")
        p_hi_ready = sem("p_hi_ready")
        p_ready = sem("p_ready")
        acc_loaded = [sem(f"acc_loaded{k}") for k in range(2)]
        acc_biased = sem("acc_biased")
        v_loaded = [sem(f"v_loaded{u}") for u in range(VU)]
        o_mm = sem("o_mm")
        acc_added = sem("acc_added")
        out_stored = [sem(f"out_stored{k}") for k in range(2)]

        BLOCKS = 2
        VTILES = 2 * PT
        STORES = NV * VU
        LOADED = (1 + (CT // 2 - 1) * STORES) * 16
        CHAIN = 7
        LINKS = NG + 5

        strip_bank = [bank[k][0:L, 0:G * L].rearrange("p (g l) -> p g l", g=G) for k in range(8)]
        out_bank = [bank[k][:, 0:G * L].rearrange("p (g l) -> p g l", g=G) for k in range(4)]

        def strips_of(a):
            return {
                ROW: a[:, :].rearrange("c (h w) -> c h w", w=W),
                COL: a[:, :].rearrange("c (h w) -> c w h", w=W),
            }

        q_strips, k_hi_strips, k_lo_strips = strips_of(q_both), strips_of(k_hi), strips_of(k_lo)
        acc_strips = [strips_of(a) for a in acc]

        def wait_alone(eng, semaphore, value):
            eng.wait_ge(semaphore, value)
            eng.sem_inc(waits_carried, 1)

        block = ctx.enter_context(nc.Block())

        @block.sync
        def _(sp):
            for k in range(2 * PT):
                sp.sem_inc(v_stored[k], 16)
            sp.dma_start(wqk_raw[:, :, :], wqkT.rearrange("(t c) o -> c t o", c=P)).then_inc(weights_loaded, 16)
            sp.dma_start(wv_raw[:, :, :], wvT.rearrange("(t c) o -> c t o", c=P)).then_inc(weights_loaded, 16)
            sp.dma_start(bqk_col[:, :], bqk.rearrange("(c u) -> c u", u=1)).then_inc(weights_loaded, 16)
            with nc.allow_non_contiguous_dma(reason="a few columns of constants"):
                sp.dma_start(bv_col[:, :], bv.rearrange("(t c) -> c t", c=P)).then_inc(weights_loaded, 16)
                sp.dma_start(gamma_col[:, :], gamma.rearrange("(a u) -> a u", u=1).broadcast_to([P, 1])).then_inc(
                    weights_loaded, 16
                )

            def load_block(b, n, s):
                sp.wait_ge(x_split, b * NB + n + 1)
                sp.dma_start(x_raw[s][:, :, :], x_blk[b, :, :, bass.ds(n * BLK, BLK)]).then_inc(x_loaded[s], 16)

            def load_next(image, done, n, s):
                sp.wait_ge(x_next_seen, done * NB + n + 1)
                sp.dma_start(x_next[s][:, :, :], x_blk[image, :, :, bass.ds(n * BLK, BLK)]).then_inc(
                    x_next_loaded[s], 16
                )

            def store_block(b, i, s):
                for j in range(PT):
                    k = s * PT + j
                    sp.wait_ge(v_ready, (b * NB + 2 * i) * PT + k + 1 + VTILES)
                    sp.dma_start(
                        vT[b, bass.ds((2 * i + s) * BLK + j * P, P), :],
                        v_out[k][:, :, :, :].rearrange("p t a c -> p (t a c)"),
                    ).then_inc(v_stored[k], 16)

            def shift_blocks(b, i):
                sp.wait_ge(qk_ready, b * NB + 2 * i + 2 + BLOCKS)
                px = bass.ds(2 * i * BLK, 2 * BLK)
                sp.dma_start(q_both[CQ:P, px], q_low[:, px]).then_inc(qk_shifted, 16)
                sp.dma_start(k_hi[0:CQ, px], k_hi[CQ:P, px]).then_inc(qk_shifted, 16)
                sp.dma_start(k_lo[0:CQ, px], k_lo[CQ:P, px]).then_inc(qk_shifted, 16)

            with sp.Fori(0, NB // 2) as i:
                for s in range(2):
                    load_next(0, 0, 2 * i + s, s)

            with sp.Fori(0, B) as b:
                for s in range(2):
                    load_block(b, s, s)
                wait_alone(sp, out_stored[1], b * (CT // 2 * STORES * 16) + 16)
                wait_alone(sp, o_mm, b * (2 * PH3) + 2 * VU)
                for s in range(2):
                    load_next((b + 1) % B, b + 1, s, s)
                with sp.Fori(0, NB // 2 - 1) as i:
                    for s in range(2):
                        load_block(b, 2 * i + 2 + s, s)
                        store_block(b, i, s)
                        load_next((b + 1) % B, b + 1, 2 * i + 2 + s, s)
                    shift_blocks(b, i)
                for s in range(2):
                    store_block(b, NB // 2 - 1, s)
                shift_blocks(b, NB // 2 - 1)
                sp.wait_ge(s_ready, (b + 1) * (2 * NG))
                for k in range(2):
                    sp.dma_start(acc[k][:, :], x_acc[b, k, :, :]).then_inc(acc_loaded[k], 16)
                for k in range(2 * PT):
                    wait_alone(sp, v_stored[k], (b + 1) * (NB // 2 * 16) + 16)
                with sp.Fori(0, CT // 2) as tp:
                    for par in range(2):
                        for o in (COL, ROW):
                            with sp.Fori(0, NV) as i:
                                n3 = ((b * CT + tp * 2 + par) * 2 + (1 - o)) * NV + i
                                for u in range(VU):
                                    if u == 4:
                                        sp.wait_ge(p_ready, (b + 1) * (2 * NG) + U)
                                    sp.wait_ge(o_mm, (n3 * VU + u) * 2 + 2)
                                    sp.dma_start(
                                        v_in[u][:, :, :, :].rearrange("p s a c -> p s (a c)"),
                                        vT_load[o][b, tp * 2 + par, :, bass.ds((i * VU + u) * VS, VS), :],
                                    ).then_inc(v_loaded[u], 16)
            for k in range(2):
                sp.wait_ge(out_stored[k], B * (CT // 2 * STORES * 16) + 16)

        @block.gpsimd
        def _(pool):
            pool.sem_inc(qk_ready, BLOCKS)
            nc.gpsimd.memset(ident[:, :], 0.0).then_inc(ident_zero, 1)
            nc.gpsimd.memset(diag_bf[:, :, :], 0.0).then_inc(ident_zero, 1)
            pool.wait_ge(ident_zero, 2)
            nc.gpsimd.affine_select(
                out=ident[:, :], in_=ident[:, :], compare_op=ALU.not_equal, fill=1.0, base=0,
                pattern=[[-1, L]], channel_multiplier=1,
            ).then_inc(consts_set, 1)
            nc.gpsimd.affine_select(
                out=diag_bf[:, :, :], in_=diag_bf[:, :, :], compare_op=ALU.not_equal, fill=MASKED, base=0,
                pattern=[[0, G], [-1, L]], channel_multiplier=1,
            ).then_inc(consts_set, 1)
            pool.wait_ge(consts_set, 2)
            nc.gpsimd.tensor_copy(ident_bf[:, :], ident[:, :]).then_inc(consts_set, 1)
            pool.wait_ge(consts_set, 3)
            pool.wait_ge(wmax_own_ready, 1)
            nc.gpsimd.partition_all_reduce(wmax[:, :], wmax_own[:, :], P, RMAX).then_inc(wmax_ready, 1)
            pool.wait_ge(wmax_ready, 1)
            pool.wait_ge(xmax_own_ready, 1)
            nc.gpsimd.partition_all_reduce(xmax[:, :], xmax_own[:, :], P, RMAX).then_inc(xmax_ready, 1)
            pool.wait_ge(xmax_ready, 1)

            def low_qk(b, n, s):
                pool.wait_ge(qk_hi_ready, b * NB + n + 1)
                px = bass.ds(n * BLK, BLK)
                nc.gpsimd.tensor_tensor(q_low[:, px], qk_f32[s][0:CQ, :], q_both[0:CQ, px], ALU.subtract)
                nc.gpsimd.tensor_tensor(
                    k_lo[CQ:P, px], qk_f32[s][CQ:P, :], k_hi[CQ:P, px], ALU.subtract
                ).then_inc(qk_ready, 1)

            with pool.Fori(0, B) as b:
                wait_alone(pool, out_stored[1], b * (CT // 2 * STORES * 16) + 16)
                with pool.Fori(0, NB // 2) as i:
                    for s in range(2):
                        low_qk(b, 2 * i + s, s)
                wait_alone(pool, qk_ready, (b + 1) * NB + BLOCKS)
                wait_alone(pool, xmax_own_ready, b + 2)
                nc.gpsimd.partition_all_reduce(xmax[:, :], xmax_own[:, :], P, RMAX).then_inc(xmax_ready, 1)
                wait_alone(pool, xmax_ready, b + 2)
                for o in (COL, ROW):
                    if o == COL:
                        wait_alone(pool, factors_ready, b + 1)
                    else:
                        wait_alone(pool, factor_row_ready, b + 1)
                    with pool.Fori(0, NI) as i:
                        for u in range(U):
                            pool.wait_ge(pT_ready, (b * 2 + 1 - o) * NG + i * U + u + 1)
                            strips = bass.ds((i * U + u) * G, G)
                            nc.gpsimd.tensor_tensor(
                                e_grp[u][:, :, :], prob[o][:, strips, :],
                                factor[o][:, strips].unsqueeze(2).to_broadcast([L, G, L]), ALU.mult,
                            ).then_inc(e_grp_ready, 1)

        @block.scalar
        def _(act):
            act.sem_inc(e_ready, U)
            for k in range(2):
                act.sem_inc(out_stored[k], 16)
            act.wait_ge(weights_loaded, 5 * 16)
            nc.scalar.copy(wqk_hi[:, :, :], wqk_raw[:, :, :]).then_inc(hi_ready, 1)
            nc.scalar.copy(wv_hi[:, :, :], wv_raw[:, :, :]).then_inc(hi_ready, 1)

            def split_hi(b, n, s, sem_round):
                act.wait_ge(x_loaded[s], sem_round)
                act.wait_ge(qk_mm, b * NB + n + 1)
                nc.scalar.copy(x_hi[s][:, :, :], x_raw[s][:, :, :]).then_inc(x_hi_ready, 1)

            def high_v(b, i, s):
                for j in range(PT):
                    k = s * PT + j
                    act.wait_ge(v_mm, (b * NB + 2 * i) * PT + k + 1)
                    act.wait_ge(v_stored[k], (b * (NB // 2) + i) * 16 + 16)
                    nc.scalar.activation(
                        v_out[k][:, :, 0, :], bank[k][:, :].rearrange("p (t c) -> p t c", t=CT), ACT.Copy,
                        scale=scales[:, SCALE_V:SCALE_V + 1],
                    ).then_inc(v_hi_ready, 1)

            def high_qk(b, n, s):
                act.wait_ge(qk_evac, b * NB + n + 1)
                px = bass.ds(n * BLK, BLK)
                nc.scalar.copy(q_both[0:CQ, px], qk_f32[s][0:CQ, :])
                nc.scalar.copy(k_hi[CQ:P, px], qk_f32[s][CQ:P, :]).then_inc(qk_hi_ready, 1)

            with act.Fori(0, B) as b:
                half = b * (NB // 2)
                split_hi(b, 0, 0, half * 16 + 16)
                act.wait_ge(scale_chain, (b + 1) * CHAIN)
                act.wait_ge(o_mm, b * (2 * PH3) + 2 * VU)
                wait_alone(act, out_stored[0], b * (CT // 2 * STORES * 16) + 16)
                with act.Fori(0, NB // 2 - 1) as i:
                    split_hi(b, 2 * i + 1, 1, (half + i) * 16 + 16)
                    high_v(b, i, 0)
                    high_qk(b, 2 * i, 0)
                    split_hi(b, 2 * i + 2, 0, (half + i) * 16 + 32)
                    high_v(b, i, 1)
                    high_qk(b, 2 * i + 1, 1)
                split_hi(b, NB - 1, 1, (half + NB // 2 - 1) * 16 + 16)
                for s in range(2):
                    high_v(b, NB // 2 - 1, s)
                    high_qk(b, NB - 2 + s, s)
                for k in range(2 * PT):
                    act.wait_ge(v_stored[k], (b + 1) * (NB // 2 * 16) + 16)
                act.wait_ge(qk_shifted, (b + 1) * (NB // 2 * 3 * 16))
                act.wait_ge(x_next_seen, (b + 2) * NB + BLOCKS)
                for o in (ROW, COL):
                    with act.Fori(0, NI) as i:
                        for u in range(U):
                            act.wait_ge(nmax_ready, (b * 2 + o) * NG + i * U + u + 1)
                            strips = bass.ds((i * U + u) * G, G)
                            if u % 2 == 0:
                                nc.scalar.activation(
                                    prob[o][:, strips, :], prob[o][:, strips, :], ACT.Exp
                                ).then_inc(e_ready, 1)
                                continue
                            for g in range(G):
                                strip = bass.ds((i * U + u) * G + g, 1)
                                last = nc.scalar.activation(
                                    prob[o][:, strip, :], strip_bank[u][:, g:g + 1, :], ACT.Exp,
                                    scale=scales[0:L, S_FACTOR:S_FACTOR + 1], bias=nmax[o][:, strip],
                                    accum_out=esum[o][:, strip],
                                )
                            last.then_inc(e_ready, 1)
                act.wait_ge(shift_ready, b + 1)
                nc.scalar.activation(scaled[:, :, :], shift[:, :, :], ACT.Exp).then_inc(shift_exp, 1)
                for o in (COL, ROW):
                    with act.Fori(0, NI) as i:
                        for u in range(U):
                            act.wait_ge(pT_ready, (b * 2 + 1 - o) * NG + i * U + u + 1 + U)
                            nc.scalar.activation(
                                parts[o][:, bass.ds((i * U + u) * G, G), 0, :], strip_bank[4 + u][:, :, :], ACT.Copy,
                                scale=TOP,
                            ).then_inc(p_hi_ready, 1)
                def add_bias(t):
                    a = acc[t % 2][:, :]
                    act.wait_ge(acc_loaded[t % 2], b * LOADED + 16 + t // 2 * STORES * 16)
                    nc.scalar.activation(a, a, ACT.Identity, bias=gbv_col[:, t:t + 1]).then_inc(acc_biased, 1)

                add_bias(0)
                for t in range(CT):
                    k = t % 2
                    n3 = (b * CT + t) * 2 * NV
                    if 0 < t < CT - 1:
                        before = b * (CT // 2) + (t - 1) // 2 + 1
                        wait_alone(act, out_stored[1 - k], before * (STORES * 16) + 16)
                        with act.Fori(0, NV) as i:
                            for u in range(VU):
                                act.wait_ge(acc_added, ((n3 + i) * VU + u) * 2 + 1 + 4)
                                px = bass.ds((i * VU + u) * (VS * W), VS * W)
                                act.dma_start(acc[1 - k][:, px], x_acc[b, t + 1, :, px]).then_inc(acc_loaded[1 - k], 16)
                    if t < CT - 1:
                        add_bias(t + 1)
                    with act.Fori(0, NV) as i:
                        for u in range(VU):
                            act.wait_ge(acc_added, ((n3 + NV + i) * VU + u) * 2 + 2 + 4)
                            px = bass.ds((i * VU + u) * (VS * W), VS * W)
                            act.dma_start(out_acc[b, t, :, px], acc[k][:, px]).then_inc(out_stored[k], 16)

        @block.vector
        def _(dve):
            dve.sem_inc(x_split, BLOCKS)
            dve.sem_inc(x_next_seen, BLOCKS)
            dve.sem_inc(v_ready, VTILES)
            dve.sem_inc(acc_added, 4)
            dve.sem_inc(p_ready, U)
            dve.wait_ge(hi_ready, 1)
            nc.vector.tensor_tensor(
                wqk_lo[:, :, :], wqk_raw[:, :, :], wqk_hi[:, :, :].bitcast(F32), ALU.subtract
            ).then_inc(weights_split, 1)
            dve.wait_ge(hi_ready, 2)
            nc.vector.tensor_tensor(
                wv_lo[:, :, :], wv_raw[:, :, :], wv_hi[:, :, :].bitcast(F32), ALU.subtract
            ).then_inc(weights_split, 1)
            nc.vector.tensor_scalar(gbv_col[:, :], bv_col[:, :], gamma_col[:, 0:1], None, ALU.mult).then_inc(
                const_chain, 1
            )
            for k, src in enumerate((wqk_raw[:, :, :], wv_raw[:, :, :])):
                nc.vector.tensor_reduce(
                    bound[:, k:k + 1], src, mybir.AxisListType.XY, ALU.max, apply_absolute_value=True
                ).then_inc(const_chain, 1)
            nc.vector.tensor_reduce(wmax_own[:, 2:3], bqk_col[:, :], AX_X, ALU.max, apply_absolute_value=True)
            dve.wait_ge(const_chain, 3)
            nc.vector.tensor_scalar(wmax_own[:, 0:2], bound[:, :], float(C), None, ALU.mult).then_inc(wmax_own_ready, 1)

            def see_next(done, n, s, sem_round):
                dve.wait_ge(x_next_loaded[s], sem_round)
                nc.vector.tensor_reduce(
                    xmax_blk[:, bass.ds(n, 1)], x_next[s][:, :, :], mybir.AxisListType.XY, ALU.max,
                    apply_absolute_value=True,
                ).then_inc(x_next_seen, 1)

            def make_scales(b):
                def step(k, ins):
                    ins.then_inc(scale_chain, 1)
                    dve.wait_ge(scale_chain, b * CHAIN + k)

                dve.wait_ge(x_next_seen, (b + 1) * NB + BLOCKS)
                nc.vector.tensor_reduce(xmax_own[:, :], xmax_blk[:, :], AX_X, ALU.max).then_inc(xmax_own_ready, 1)
                dve.wait_ge(xmax_ready, b + 1)
                nc.vector.tensor_scalar(bound[:, 1:2], xmax[:, :], wmax[:, 1:2], TINY, ALU.mult, ALU.max)
                step(1, nc.vector.tensor_scalar(bound[:, 0:1], xmax[:, :], wmax[:, 0:1], wmax[:, 2:3], ALU.mult, ALU.add))
                step(2, nc.vector.tensor_scalar(bound[:, 0:1], bound[:, 0:1], TINY, None, ALU.max))
                step(3, nc.vector.tensor_scalar(
                    floor2[:, :].bitcast(I32), bound[:, :].bitcast(I32), EXPONENT, None, ALU.bitwise_and
                ))
                step(4, nc.vector.tensor_scalar(unscale[:, :], floor2[:, :], 1.0 / TOP, None, ALU.mult))
                step(5, nc.vector.reciprocal(scales_next[:, SCALE_QK:SCALE_V + 1], unscale[:, :]))
                nc.vector.tensor_scalar(
                    scales_next[:, BIAS_QK:BIAS_QK + 1], bqk_col[:, :], scales_next[:, SCALE_QK:SCALE_QK + 1], None,
                    ALU.mult,
                )
                nc.vector.tensor_scalar(
                    scales_next[:, S_FACTOR:S_FACTOR + 1], unscale[:, 0:1], unscale[:, 0:1], None, ALU.mult
                )
                step(6, nc.vector.tensor_scalar(
                    scales_next[:, O_FACTOR:O_FACTOR + 1], unscale[:, 1:2], gamma_col[:, 0:1], 1.0 / TOP,
                    ALU.mult, ALU.mult,
                ))

            def split_lo(b, n, s):
                dve.wait_ge(x_hi_ready, b * NB + n + 1)
                nc.vector.tensor_tensor(
                    x_lo[s][:, :, :], x_raw[s][:, :, :], x_hi[s][:, :, :].bitcast(F32), ALU.subtract
                ).then_inc(x_split, 1)

            def low_v(b, i, s):
                for j in range(PT):
                    k = s * PT + j
                    dve.wait_ge(v_hi_ready, (b * NB + 2 * i) * PT + k + 1)
                    nc.vector.scalar_tensor_tensor(
                        out=v_out[k][:, :, 1, :], in0=bank[k][:, :].rearrange("p (t c) -> p t c", t=CT),
                        scalar=scales[:, SCALE_V:SCALE_V + 1], in1=v_out[k][:, :, 0, :], op0=ALU.mult, op1=ALU.subtract,
                    ).then_inc(v_ready, 1)

            def evac_qk(b, n, s):
                dve.wait_ge(qk_mm, b * NB + n + 1 + BLOCKS)
                dve.wait_ge(qk_ready, b * NB + n + 1)
                nc.vector.tensor_scalar(
                    qk_f32[s][:, :], bank[4 + s][:, 0:BLK], scales[:, SCALE_QK:SCALE_QK + 1],
                    scales[:, BIAS_QK:BIAS_QK + 1],
                    ALU.mult, ALU.add,
                ).then_inc(qk_evac, 1)

            with dve.Fori(0, NB // 2) as i:
                for s in range(2):
                    see_next(0, 2 * i + s, s, i * 16 + 16)
            dve.wait_ge(wmax_ready, 1)
            make_scales(0)

            with dve.Fori(0, B) as b:
                dve.wait_ge(acc_added, b * (2 * PH3) + 4)
                nc.vector.tensor_copy(scales[:, :], scales_next[:, :]).then_inc(scale_chain, 1)
                dve.wait_ge(scale_chain, (b + 1) * CHAIN)
                split_lo(b, 0, 0)
                nxt = (b + 1) * (NB // 2)
                with dve.Fori(0, NB // 2 - 1) as i:
                    for s in range(2):
                        split_lo(b, 2 * i + 1 + s, 1 - s)
                        low_v(b, i, s)
                        evac_qk(b, 2 * i + s, s)
                        see_next(b + 1, 2 * i + s, s, (nxt + i) * 16 + 16)
                split_lo(b, NB - 1, 1)
                for s in range(2):
                    low_v(b, NB // 2 - 1, s)
                    evac_qk(b, NB - 2 + s, s)
                    see_next(b + 1, NB - 2 + s, s, (nxt + NB // 2 - 1) * 16 + 16)
                make_scales(b + 1)
                for k in range(2 * PT):
                    wait_alone(dve, v_stored[k], (b + 1) * (NB // 2 * 16) + 16)
                for o in (ROW, COL):
                    with dve.Fori(0, NI) as i:
                        def group(u):
                            return (b * 2 + o) * NG + i * U + u, bass.ds((i * U + u) * G, G)

                        def sum_e(u):
                            n, strips = group(u)
                            dve.wait_ge(e_ready, n + 1 + U)
                            nc.vector.tensor_reduce(
                                esum[o][:, strips], prob[o][:, strips, :], AX_X, ALU.add
                            ).then_inc(esum_even, 1)

                        for u in range(U):
                            n, strips = group(u)
                            dve.wait_ge(s_ready, n + 1)
                            nc.vector.tensor_reduce(
                                nmax[o][:, strips], strip_bank[u][:, :, :], AX_X, ALU.max, negate=True
                            ).then_inc(nmax_raw, 1)
                            dve.wait_ge(nmax_raw, n + 1)
                            last = nc.vector.tensor_scalar(
                                nmax[o][:, strips], nmax[o][:, strips], scales[0:L, S_FACTOR:S_FACTOR + 1], None, ALU.mult
                            )
                            if u % 2 == 0:
                                last.then_inc(dve_chain, 1)
                                dve.wait_ge(dve_chain, b * LINKS + (o * NI + i) * 2 + u // 2 + 1)
                                last = nc.vector.scalar_tensor_tensor(
                                    out=prob[o][:, strips, :], in0=strip_bank[u][:, :, :],
                                    scalar=scales[0:L, S_FACTOR:S_FACTOR + 1],
                                    in1=nmax[o][:, strips].unsqueeze(2).to_broadcast([L, G, L]),
                                    op0=ALU.mult, op1=ALU.add,
                                )
                            last.then_inc(nmax_ready, 1)
                            if u % 2:
                                sum_e(u - 1)
                link = b * LINKS + NG
                dve.wait_ge(stats_T, b + 1)
                row_nmax, row_esum = bank[0][0:L, 0:L], bank[1][0:L, 0:L]
                nc.vector.tensor_tensor(njoint[:, :], row_nmax, nmax[COL][:, :], ALU.min).then_inc(dve_chain, 1)
                dve.wait_ge(dve_chain, link + 1)
                nc.vector.tensor_tensor(shift[:, ROW, :], njoint[:, :], row_nmax, ALU.subtract)
                nc.vector.tensor_tensor(shift[:, COL, :], njoint[:, :], nmax[COL][:, :], ALU.subtract).then_inc(
                    shift_ready, 1
                )
                dve.wait_ge(shift_exp, b + 1)
                nc.vector.tensor_tensor(shift[:, ROW, :], scaled[:, ROW, :], row_esum, ALU.mult).then_inc(dve_chain, 1)
                nc.vector.tensor_tensor(shift[:, COL, :], scaled[:, COL, :], esum[COL][:, :], ALU.mult).then_inc(
                    dve_chain, 1
                )
                dve.wait_ge(dve_chain, link + 3)
                nc.vector.tensor_tensor(njoint[:, :], shift[:, ROW, :], shift[:, COL, :], ALU.add).then_inc(dve_chain, 1)
                dve.wait_ge(dve_chain, link + 4)
                nc.vector.reciprocal(shift[:, ROW, :], njoint[:, :]).then_inc(dve_chain, 1)
                dve.wait_ge(dve_chain, link + 5)
                nc.vector.tensor_tensor(factor_rowT[:, :], scaled[:, ROW, :], shift[:, ROW, :], ALU.mult)
                nc.vector.tensor_tensor(factor[COL][:, :], scaled[:, COL, :], shift[:, ROW, :], ALU.mult).then_inc(
                    factors_ready, 1
                )
                dve.wait_ge(factor_T, b + 1)
                nc.vector.tensor_copy(factor[ROW][:, :], bank[2][0:L, 0:L]).then_inc(factor_row_ready, 1)
                for o in (COL, ROW):
                    with dve.Fori(0, NI) as i:
                        for u in range(U):
                            dve.wait_ge(p_hi_ready, (b * 2 + 1 - o) * NG + i * U + u + 1)
                            strips = bass.ds((i * U + u) * G, G)
                            nc.vector.scalar_tensor_tensor(
                                out=parts[o][:, strips, 1, :], in0=strip_bank[4 + u][:, :, :], scalar=TOP,
                                in1=parts[o][:, strips, 0, :], op0=ALU.mult, op1=ALU.subtract,
                            ).then_inc(p_ready, 1)
                with dve.Fori(0, CT // 2) as tp:
                    for par in range(2):
                        for o in (COL, ROW):
                            first = ((b * CT + tp * 2 + par) * 2 + (1 - o)) * NV
                            with dve.Fori(0, NV) as i:
                                if o == COL:
                                    dve.wait_ge(acc_biased, b * CT + tp * 2 + par + 1)
                                else:
                                    dve.wait_ge(acc_added, first * (2 * VU) + 4)
                                for u in range(VU):
                                    for half in range(2):
                                        n = ((first + i) * VU + u) * 2 + half
                                        dve.wait_ge(o_mm, n + 1 + 2 * VU)
                                        strips = bass.ds(((i * VU + u) * 2 + half) * G, G)
                                        a = acc_strips[par][o][:, strips, :]
                                        nc.vector.scalar_tensor_tensor(
                                            out=a, in0=out_bank[(2 * u + half) % 4], scalar=scales[:, O_FACTOR:O_FACTOR + 1],
                                            in1=a, op0=ALU.mult, op1=ALU.add,
                                        ).then_inc(acc_added, 1)

        @block.tensor
        def _(pe):
            pe.sem_inc(qk_mm, BLOCKS)
            pe.sem_inc(pT_ready, U)
            pe.sem_inc(o_mm, 2 * VU)
            pe.wait_ge(weights_split, 2)
            pe.wait_ge(consts_set, 3)

            def three_products(dst, stationary, moving):
                for t in range(CT):
                    (s_hi, s_lo), (m_hi, m_lo) = stationary(t), moving(t)
                    nc.tensor.matmul(dst, s_hi, m_hi, start=(t == 0), stop=False)
                    nc.tensor.matmul(dst, s_hi, m_lo, start=False, stop=False)
                    last = nc.tensor.matmul(dst, s_lo, m_hi, start=False, stop=(t == CT - 1))
                return last

            with pe.Fori(0, B) as b:
                wait_alone(pe, acc_added, b * (2 * PH3) + 4)
                with pe.Fori(0, NB // 2) as i:
                    for s in range(2):
                        n = b * NB + 2 * i + s
                        pe.wait_ge(x_split, n + 1 + BLOCKS)
                        for j in range(PT):
                            k = s * PT + j
                            px = slice(j * P, (j + 1) * P)
                            pe.wait_ge(v_ready, (b * NB + 2 * i) * PT + k + 1)
                            three_products(
                                bank[k][:, :],
                                lambda t: (x_hi[s][:, t, px], x_lo[s][:, t, px]),
                                lambda t: (wv_hi[:, t, :], wv_lo[:, t, :]),
                            ).then_inc(v_mm, 1)
                        pe.wait_ge(qk_ready, n + 1)
                        three_products(
                            bank[4 + s][:, 0:BLK],
                            lambda t: (wqk_hi[:, t, :], wqk_lo[:, t, :]),
                            lambda t: (x_hi[s][:, t, :], x_lo[s][:, t, :]),
                        ).then_inc(qk_mm, 1)
                pe.wait_ge(qk_shifted, (b + 1) * (NB // 2 * 3 * 16))
                pe.wait_ge(qk_ready, (b + 1) * NB + BLOCKS)
                wait_alone(pe, v_ready, (b + 1) * (NB * PT) + VTILES)
                for o in (ROW, COL):
                    with pe.Fori(0, NI) as i:
                        strips = bass.ds(i * (U * G), U * G)
                        q, k_h, k_l = q_strips[o][:, strips, :], k_hi_strips[o][:, strips, :], k_lo_strips[o][:, strips, :]
                        for u in range(U):
                            pe.wait_ge(e_ready, (b * 2 + o) * NG + i * U + u + 1)
                            for g in range(G):
                                strip = u * G + g
                                nc.tensor.matmul(
                                    strip_bank[u][:, g, :], q[:, strip, :], k_h[:, strip, :],
                                    start=(o == ROW or g == 0), stop=False,
                                )
                                last = nc.tensor.matmul(
                                    strip_bank[u][:, g, :], q[:, strip, :], k_l[:, strip, :],
                                    start=False, stop=(o == ROW),
                                )
                            if o == COL:
                                last = nc.tensor.matmul(
                                    strip_bank[u], ident_bf[:, :], diag_bf[:, :, :], start=False, stop=True
                                )
                            last.then_inc(s_ready, 1)
                pe.wait_ge(e_ready, (b + 1) * (2 * NG) + U)
                pe.wait_ge(esum_even, (b + 1) * NG)
                nc.tensor.transpose(bank[0][0:L, 0:L], nmax[ROW][:, :], ident[:, :])
                nc.tensor.transpose(bank[1][0:L, 0:L], esum[ROW][:, :], ident[:, :]).then_inc(stats_T, 1)
                pe.wait_ge(factors_ready, b + 1)
                nc.tensor.transpose(bank[2][0:L, 0:L], factor_rowT[:, :], ident[:, :]).then_inc(factor_T, 1)
                for o in (COL, ROW):
                    with pe.Fori(0, NI) as i:
                        for u in range(U):
                            n = (b * 2 + 1 - o) * NG + i * U + u
                            pe.wait_ge(e_grp_ready, n + 1)
                            pe.wait_ge(p_ready, n + 1)
                            for g in range(G):
                                last = nc.tensor.transpose(
                                    strip_bank[4 + u][:, g, :], e_grp[u][:, g, :], ident[:, :]
                                )
                            last.then_inc(pT_ready, 1)
                wait_alone(pe, p_ready, (b + 1) * (2 * NG) + U)
                with pe.Fori(0, CT) as t:
                    for o in (COL, ROW):
                        n3 = ((b * CT + t) * 2 + (1 - o)) * NV
                        for load in range(NV * VU):
                            i, u = divmod(load, VU)
                            pe.wait_ge(v_loaded[u], (n3 + i) * 16 + 16)
                            for half in range(2):
                                pe.wait_ge(acc_added, (n3 * VU + load) * 2 + half + 1)
                                dst = out_bank[(2 * load + half) % 4]
                                for g in range(G):
                                    strip = (load * 2 + half) * G + g
                                    for a in range(2):
                                        v = v_in[u][:, half * G + g, a, :]
                                        for c in range(2):
                                            last = nc.tensor.matmul(
                                                dst[:, g, :], v, parts[o][:, strip, c, :],
                                                start=(a == 0 and c == 0), stop=(a == 1 and c == 1),
                                            )
                                last.then_inc(o_mm, 1)


def kernel(x, L0_conv_Wq, L0_conv_bq, L0_conv_Wk, L0_conv_bk, L0_conv_Wv, L0_conv_bv, L0_conv_gamma):
    import numpy as np
    import concourse.bacc as bacc
    from concourse.bass_utils import run_bass_kernel_spmd

    arrays = {
        "x": np.ascontiguousarray(x),
        "wqkT": np.ascontiguousarray(np.concatenate([np.asarray(L0_conv_Wq), np.asarray(L0_conv_Wk)], axis=0).T),
        "wvT": np.ascontiguousarray(np.asarray(L0_conv_Wv).T),
        "bqk": np.concatenate([np.asarray(L0_conv_bq), np.asarray(L0_conv_bk)]),
        "bv": np.ascontiguousarray(L0_conv_bv),
        "gamma": np.ascontiguousarray(L0_conv_gamma),
    }
    nc = bacc.Bacc("TRN2", target_bir_lowering=False, num_devices=1)
    args = [
        nc.dram_tensor(n, a.shape, mybir.dt.from_np(a.dtype), kind="ExternalInput").ap() for n, a in arrays.items()
    ]
    out = nc.dram_tensor("out", arrays["x"].shape, F32, kind="ExternalOutput").ap()
    criss_cross_attention(nc, *args, out)
    return run_bass_kernel_spmd(nc, [arrays], core_ids=[0]).results[0]["out"]
```

```python
from contextlib import ExitStack

import concourse.bass as bass
from concourse import mybir

F32 = mybir.dt.float32
F32R = mybir.dt.float32r
F16 = mybir.dt.float16
BF16 = mybir.dt.bfloat16
I32 = mybir.dt.int32
ALU = mybir.AluOpType
ACT = mybir.ActivationFunctionType
AX_X = mybir.AxisListType.X

RMAX = bass.bass_isa.ReduceOp.max

P = 128
EXPONENT = 0x7F800000
TOP = 2.0 ** 14
TINY = 2.0 ** -40
MASKED = -1e38
ROW, COL = 0, 1


def criss_cross_attention(nc, x, wqkT, wvT, bqk, bv, gamma, out):
    B, C, H, W = x.shape
    L = H
    assert H == W and C % P == 0 and L <= P
    HW = H * W
    CT = C // P
    CQ = wqkT.shape[1] // 2
    assert 2 * CQ == P

    BLK = 256
    PT = BLK // P
    NB = HW // BLK
    assert NB % 2 == 0 and HW % BLK == 0

    G = 4
    NG = L // G
    NP = NG // 2
    SP = 4
    NS = NP // SP

    BODY = 2 * (2 * G * W) // (2 * BLK)
    NJ = NB // 2 // BODY
    assert BODY * 2 * BLK == 2 * (2 * G * W) and NJ * BODY * 2 == NB and 2 * NJ == NP
    U = 4
    NI = NG // U
    assert NG % U == 0 and G * L * 4 <= 2048

    VS = 2 * G
    VU = 6
    NV = L // VS // VU
    assert L % (VS * VU) == 0
    PH3 = CT * 2 * NV * VU

    x_blk = x.rearrange("b (t c) h w -> b c t (h w)", c=P)
    x_acc = x.rearrange("b (t c) h w -> b t c (h w)", c=P)
    out_acc = out.rearrange("b (t c) h w -> b t c (h w)", c=P)
    vT = nc.dram_tensor("v_pixel_major", [B, HW, CT * 2 * P], F16, kind="Internal").ap()
    vT_load = {
        ROW: vT.rearrange("b (h w) (t a) -> b t w h a", w=W, t=CT),
        COL: vT.rearrange("b (h w) (t a) -> b t h w a", w=W, t=CT),
    }

    base = [(nc.sbuf_base + 63) // 64 * 64]

    def place(name, shape, dt, at=None):
        size = 1
        for n in shape[1:]:
            size *= n
        size *= 2 if dt in (BF16, F16) else 4
        where = base[0] if at is None else at
        t = nc.alloc_sbuf_tensor_at(name, shape, dt, offset=where)
        if at is None:
            step = 64 if size >= 64 else 32
            base[0] += (size + step - 1) // step * step
        return t, where

    acc0, acc0_at = place("acc0", [P, HW], F32)
    acc1, acc1_at = place("acc1", [P, HW], F32)
    acc = [acc0, acc1]
    q_both, _ = place("q_both", [P, HW], F16, at=acc0_at)
    k_hi, _ = place("k_hi", [P, HW], F16, at=acc0_at + 2 * HW)
    k_lo, _ = place("k_lo", [P, HW], F16, at=acc1_at)
    prob_row, prob_row_at = place("prob_row", [L, L, L], F32)
    prob_col, prob_col_at = place("prob_col", [L, L, L], F32)
    prob = {ROW: prob_row, COL: prob_col}
    parts = {
        o: prob[o][:, :, :].bitcast(F16).rearrange("p s (a q) -> p s a q", a=2) for o in (ROW, COL)
    }
    wqk_raw, _ = place("wqk_raw", [P, CT, P], F32, at=prob_row_at)
    wv_raw, _ = place("wv_raw", [P, CT, C], F32, at=prob_row_at + CT * P * 4)
    wqk_hi, _ = place("wqk_hi", [P, CT, P], F32R)
    wqk_lo, _ = place("wqk_lo", [P, CT, P], F32R)
    wv_hi, _ = place("wv_hi", [P, CT, C], F32R)
    wv_lo, _ = place("wv_lo", [P, CT, C], F32R)
    FIRST = 6
    first_at = prob_row_at + CT * (P + C) * 4
    x_first = [place(f"x_first{k}", [P, CT, BLK], F32, at=first_at + k * CT * BLK * 4)[0] for k in range(FIRST)]
    assert first_at + FIRST * CT * BLK * 4 <= prob_row_at + L * L * 4 and NB % FIRST == 0
    x_raw_at = base[0]
    x_raw = [place(f"x_raw{s}", [P, CT, BLK], F32)[0] for s in range(2)]
    x_hi_at = base[0]
    x_hi = [place(f"x_hi{s}", [P, CT, BLK], F32R)[0] for s in range(2)]
    x_lo_at = [0, 0]
    x_lo = [None, None]
    for s in range(2):
        x_lo[s], x_lo_at[s] = place(f"x_lo{s}", [P, CT, BLK], F32R)
    at = prob_col_at
    v_out, qk_f32, x_next = [], [], []
    for k in range(2 * PT):
        v_out.append(place(f"v_out{k}", [P, CT, 2, P], F16, at=at)[0])
        at += C * 4
    for k in range(2):
        x_next.append(place(f"x_next{k}", [P, CT, BLK], F32, at=at)[0])
        at += CT * BLK * 4
    for k in range(2):
        qk_f32.append(place(f"qk_f32{k}", [P, BLK], F32, at=at)[0])
        at += BLK * 4
    q_low, _ = place("q_low", [CQ, HW], F16, at=at)
    assert at + HW * 2 <= prob_col_at + L * L * 4
    assert VS * 2 * P * 2 == CT * BLK * 4
    v_in = [place(f"v_in{u}", [L, VS, 2, P], F16)[0] for u in range(2)]
    v_in += [place(f"v_in{2 + s}", [L, VS, 2, P], F16, at=x_lo_at[s])[0] for s in range(2)]
    v_in += [place(f"v_in{u}", [L, VS, 2, P], F16)[0] for u in range(4, VU)]
    e_grp = [place(f"e_grp{u}", [L, G, L], F32, at=x_hi_at + u * G * L * 4)[0] for u in range(U)]
    assert U * G * L * 4 <= 2 * CT * BLK * 4
    nmax, factor = {}, {}
    for o in (ROW, COL):
        nmax[o], at = place(f"nmax{o}", [L, L], F32)
        factor[o], _ = place(f"factor{o}", [L, L], F32, at=at)
    esum = {o: place(f"esum{o}", [L, L], F32)[0] for o in (ROW, COL)}
    ident, _ = place("ident", [L, L], F32)
    ident_bf, _ = place("ident_bf", [L, L], BF16)
    diag_bf, _ = place("diag_bf", [L, G, L], BF16)
    at = x_raw_at
    njoint, _ = place("njoint", [L, L], F32, at=at)
    shift, _ = place("shift", [L, 2, L], F32, at=at + L * 4)
    scaled, _ = place("scaled", [L, 2, L], F32, at=at + 3 * L * 4)
    factor_rowT, _ = place("factor_rowT", [L, L], F32, at=at + 5 * L * 4)
    bqk_col, _ = place("bqk_col", [P, 1], F32)
    bv_col, _ = place("bv_col", [P, CT], F32)
    gamma_col, _ = place("gamma_col", [P, 1], F32)
    gbv_col, _ = place("gbv_col", [P, CT], F32)
    wmax_own, _ = place("wmax_own", [P, 3], F32)
    wmax, _ = place("wmax", [P, 3], F32)
    xmax_blk, _ = place("xmax_blk", [P, NB], F32)
    xmax_own, _ = place("xmax_own", [P, 1], F32)
    xmax, _ = place("xmax", [P, 1], F32)
    bound, _ = place("bound", [P, 2], F32)
    floor2, _ = place("floor2", [P, 2], F32)
    unscale, _ = place("unscale", [P, 2], F32)
    SCALE_QK, SCALE_V, BIAS_QK, S_FACTOR, O_FACTOR = range(5)
    scales, _ = place("scales", [P, 5], F32)
    scales_next, _ = place("scales_next", [P, 5], F32)
    assert base[0] <= nc.sbuf_usable_end

    with ExitStack() as ctx:
        pair = [ctx.enter_context(nc.psum_tensor(f"banks{2 * k}{2 * k + 1}", [P, 2, 512], F32)) for k in range(4)]
        bank = [pair[k // 2][:, k % 2, :] for k in range(8)]

        def sem(name):
            return ctx.enter_context(nc.semaphore(name))

        weights_loaded = sem("weights_loaded")
        consts_set = sem("consts_set")
        ident_zero = sem("ident_zero")
        hi_ready = sem("hi_ready")
        weights_split = sem("weights_split")
        wmax_own_ready = sem("wmax_own_ready")
        wmax_ready = sem("wmax_ready")
        const_chain = sem("const_chain")
        waits_carried = sem("waits_carried")
        x_next_loaded = [sem(f"x_next_loaded{s}") for s in range(2)]
        x_next_seen = sem("x_next_seen")
        x_first_loaded = [sem(f"x_first_loaded{s}") for s in range(FIRST)]
        x_first_seen = sem("x_first_seen")
        xmax_own_ready = sem("xmax_own_ready")
        xmax_ready = sem("xmax_ready")
        scale_chain = sem("scale_chain")
        x_loaded = [sem(f"x_loaded{s}") for s in range(2)]
        x_hi_ready = sem("x_hi_ready")
        x_split = sem("x_split")
        qk_mm = sem("qk_mm")
        v_mm = sem("v_mm")
        v_hi_ready = sem("v_hi_ready")
        v_ready = sem("v_ready")
        v_stored = [sem(f"v_stored{k}") for k in range(2 * PT)]
        qk_evac = sem("qk_evac")
        qk_hi_ready = sem("qk_hi_ready")
        qk_ready = sem("qk_ready")
        qk_shifted = [sem(f"qk_shifted{d}") for d in range(BODY)]
        s_ready = sem("s_ready")
        nmax_raw = sem("nmax_raw")
        nmax_ready = sem("nmax_ready")
        s_shifted = sem("s_shifted")
        e_ready = sem("e_ready")
        esum_even = sem("esum_even")
        stats_T = sem("stats_T")
        shift_ready = sem("shift_ready")
        shift_exp = sem("shift_exp")
        factors_ready = sem("factors_ready")
        factor_T = sem("factor_T")
        factor_row_ready = sem("factor_row_ready")
        dve_chain = sem("dve_chain")
        e_grp_ready = sem("e_grp_ready")
        pT_ready = sem("pT_ready")
        p_hi_ready = sem("p_hi_ready")
        p_ready = sem("p_ready")
        acc_loaded = [sem(f"acc_loaded{k}") for k in range(2)]
        bias_added = sem("bias_added")
        v_loaded = [sem(f"v_loaded{u}") for u in range(VU)]
        o_mm = sem("o_mm")
        acc_added = sem("acc_added")
        out_stored = [sem(f"out_stored{k}") for k in range(2)]

        BLOCKS = 2
        VTILES = 2 * PT
        STORES = NV * VU
        AHEAD = 2
        LOADED = (1 + (CT // 2 - 1) * STORES) * 16
        CHAIN = 7
        LINKS = 5

        strip_bank = [bank[k][0:L, 0:G * L].rearrange("p (g l) -> p g l", g=G) for k in range(8)]
        pair_strips = [pair[k][0:L, :, 0:G * L].rearrange("p u (g l) -> p u g l", g=G) for k in range(SP)]
        out_bank = [bank[k][:, 0:G * L].rearrange("p (g l) -> p g l", g=G) for k in range(4)]

        def strips_of(a):
            return {
                ROW: a[:, :].rearrange("c (h w) -> c h w", w=W),
                COL: a[:, :].rearrange("c (h w) -> c w h", w=W),
            }

        q_strips, k_hi_strips, k_lo_strips = strips_of(q_both), strips_of(k_hi), strips_of(k_lo)
        acc_strips = [strips_of(a) for a in acc]

        def wait_alone(eng, semaphore, value):
            eng.wait_ge(semaphore, value)
            eng.sem_inc(waits_carried, 1)

        block = ctx.enter_context(nc.Block())

        @block.sync
        def _(sp):
            for k in range(2 * PT):
                sp.sem_inc(v_stored[k], 16)
            sp.dma_start(wqk_raw[:, :, :], wqkT.rearrange("(t c) o -> c t o", c=P)).then_inc(weights_loaded, 16)
            sp.dma_start(wv_raw[:, :, :], wvT.rearrange("(t c) o -> c t o", c=P)).then_inc(weights_loaded, 16)
            sp.dma_start(bqk_col[:, :], bqk.rearrange("(c u) -> c u", u=1)).then_inc(weights_loaded, 16)
            with nc.allow_non_contiguous_dma(reason="a few columns of constants"):
                sp.dma_start(bv_col[:, :], bv.rearrange("(t c) -> c t", c=P)).then_inc(weights_loaded, 16)
                sp.dma_start(gamma_col[:, :], gamma.rearrange("(a u) -> a u", u=1).broadcast_to([P, 1])).then_inc(
                    weights_loaded, 16
                )

            def load_block(b, n, s):
                sp.wait_ge(x_split, b * NB + n + 1)
                sp.dma_start(x_raw[s][:, :, :], x_blk[b, :, :, bass.ds(n * BLK, BLK)]).then_inc(x_loaded[s], 16)

            def load_next(b, n, s):
                sp.wait_ge(x_next_seen, b * NB + n + 1)
                sp.dma_start(x_next[s][:, :, :], x_blk[(b + 1) % B, :, :, bass.ds(n * BLK, BLK)]).then_inc(
                    x_next_loaded[s], 16
                )

            def store_block(b, i, s):
                for j in range(PT):
                    k = s * PT + j
                    sp.wait_ge(v_ready, (b * NB + 2 * i) * PT + k + 1 + VTILES)
                    sp.dma_start(
                        vT[b, bass.ds((2 * i + s) * BLK + j * P, P), :],
                        v_out[k][:, :, :, :].rearrange("p t a c -> p (t a c)"),
                    ).then_inc(v_stored[k], 16)

            def shift_blocks(b, i, d):
                sp.wait_ge(qk_ready, b * NB + 2 * i + 2 + BLOCKS)
                px = bass.ds(2 * i * BLK, 2 * BLK)
                sp.dma_start(q_both[CQ:P, px], q_low[:, px]).then_inc(qk_shifted[d], 16)
                sp.dma_start(k_hi[0:CQ, px], k_hi[CQ:P, px]).then_inc(qk_shifted[d], 16)
                sp.dma_start(k_lo[0:CQ, px], k_lo[CQ:P, px]).then_inc(qk_shifted[d], 16)

            with sp.Fori(0, NB // FIRST) as i:
                for s in range(FIRST):
                    sp.wait_ge(x_first_seen, i * FIRST + s + 1)
                    sp.dma_start(x_first[s][:, :, :], x_blk[0, :, :, bass.ds((i * FIRST + s) * BLK, BLK)]).then_inc(
                        x_first_loaded[s], 16
                    )

            with sp.Fori(0, B) as b:
                for s in range(2):
                    load_block(b, s, s)
                wait_alone(sp, out_stored[1], b * (CT // 2 * STORES * 16) + 16)
                wait_alone(sp, o_mm, b * (2 * PH3) + 2 * VU)
                for s in range(2):
                    load_next(b, s, s)

                def double_blocks(j, last):
                    for d in range(BODY):
                        i = j * BODY + d
                        for s in range(2):
                            more = not (last and d == BODY - 1)
                            if more:
                                load_block(b, 2 * i + 2 + s, s)
                            store_block(b, i, s)
                            if more:
                                load_next(b, 2 * i + 2 + s, s)
                        shift_blocks(b, i, d)

                with sp.Fori(0, NJ - 1) as j:
                    double_blocks(j, False)
                double_blocks(NJ - 1, True)
                for k in range(2 * PT):
                    wait_alone(sp, v_stored[k], (b + 1) * (NB // 2 * 16) + 16)
                with sp.Fori(0, CT // 2) as tp:
                    for par in range(2):
                        for o in (COL, ROW):
                            with sp.Fori(0, NV) as i:
                                n3 = ((b * CT + tp * 2 + par) * 2 + (1 - o)) * NV + i
                                for u in range(VU):
                                    sp.wait_ge(o_mm, (n3 * VU + u) * 2 + 2)
                                    sp.dma_start(
                                        v_in[u][:, :, :, :].rearrange("p s a c -> p s (a c)"),
                                        vT_load[o][b, tp * 2 + par, :, bass.ds((i * VU + u) * VS, VS), :],
                                    ).then_inc(v_loaded[u], 16)
            for k in range(2):
                sp.wait_ge(out_stored[k], B * (CT // 2 * STORES * 16) + 16)

        @block.gpsimd
        def _(pool):
            pool.sem_inc(qk_ready, BLOCKS)
            nc.gpsimd.memset(ident[:, :], 0.0).then_inc(ident_zero, 1)
            nc.gpsimd.memset(diag_bf[:, :, :], 0.0).then_inc(ident_zero, 1)
            pool.wait_ge(ident_zero, 2)
            nc.gpsimd.affine_select(
                out=ident[:, :], in_=ident[:, :], compare_op=ALU.not_equal, fill=1.0, base=0,
                pattern=[[-1, L]], channel_multiplier=1,
            ).then_inc(consts_set, 1)
            nc.gpsimd.affine_select(
                out=diag_bf[:, :, :], in_=diag_bf[:, :, :], compare_op=ALU.not_equal, fill=MASKED, base=0,
                pattern=[[0, G], [-1, L]], channel_multiplier=1,
            ).then_inc(consts_set, 1)
            pool.wait_ge(consts_set, 2)
            nc.gpsimd.tensor_copy(ident_bf[:, :], ident[:, :]).then_inc(consts_set, 1)
            pool.wait_ge(consts_set, 3)
            pool.wait_ge(wmax_own_ready, 1)
            nc.gpsimd.partition_all_reduce(wmax[:, :], wmax_own[:, :], P, RMAX).then_inc(wmax_ready, 1)
            pool.wait_ge(wmax_ready, 1)
            pool.wait_ge(xmax_own_ready, 1)
            nc.gpsimd.partition_all_reduce(xmax[:, :], xmax_own[:, :], P, RMAX).then_inc(xmax_ready, 1)
            pool.wait_ge(xmax_ready, 1)

            def low_qk(b, n, s):
                pool.wait_ge(qk_hi_ready, b * NB + n + 1)
                px = bass.ds(n * BLK, BLK)
                nc.gpsimd.tensor_tensor(q_low[:, px], qk_f32[s][0:CQ, :], q_both[0:CQ, px], ALU.subtract)
                nc.gpsimd.tensor_tensor(
                    k_lo[CQ:P, px], qk_f32[s][CQ:P, :], k_hi[CQ:P, px], ALU.subtract
                ).then_inc(qk_ready, 1)

            with pool.Fori(0, B) as b:
                wait_alone(pool, out_stored[1], b * (CT // 2 * STORES * 16) + 16)
                with pool.Fori(0, NB // 2) as i:
                    for s in range(2):
                        low_qk(b, 2 * i + s, s)
                wait_alone(pool, qk_ready, (b + 1) * NB + BLOCKS)
                wait_alone(pool, xmax_own_ready, b + 2)
                nc.gpsimd.partition_all_reduce(xmax[:, :], xmax_own[:, :], P, RMAX).then_inc(xmax_ready, 1)
                wait_alone(pool, xmax_ready, b + 2)
                for o in (COL, ROW):
                    if o == COL:
                        wait_alone(pool, factors_ready, b + 1)
                    else:
                        wait_alone(pool, factor_row_ready, b + 1)
                    with pool.Fori(0, NI) as i:
                        for u in range(U):
                            pool.wait_ge(pT_ready, (b * 2 + 1 - o) * NG + i * U + u + 1)
                            strips = bass.ds((i * U + u) * G, G)
                            nc.gpsimd.tensor_tensor(
                                e_grp[u][:, :, :], prob[o][:, strips, :],
                                factor[o][:, strips].unsqueeze(2).to_broadcast([L, G, L]), ALU.mult,
                            ).then_inc(e_grp_ready, 1)

        @block.scalar
        def _(act):
            act.sem_inc(e_ready, SP)
            for k in range(2):
                act.sem_inc(out_stored[k], 16)
            act.wait_ge(weights_loaded, 5 * 16)
            nc.scalar.copy(wqk_hi[:, :, :], wqk_raw[:, :, :]).then_inc(hi_ready, 1)
            nc.scalar.copy(wv_hi[:, :, :], wv_raw[:, :, :]).then_inc(hi_ready, 1)

            def split_hi(b, n, s, sem_round):
                act.wait_ge(x_loaded[s], sem_round)
                act.wait_ge(qk_mm, b * NB + n + 1)
                nc.scalar.copy(x_hi[s][:, :, :], x_raw[s][:, :, :]).then_inc(x_hi_ready, 1)

            def high_v(b, i, s):
                for j in range(PT):
                    k = s * PT + j
                    act.wait_ge(v_mm, (b * NB + 2 * i) * PT + k + 1)
                    act.wait_ge(v_stored[k], (b * (NB // 2) + i) * 16 + 16)
                    nc.scalar.activation(
                        v_out[k][:, :, 0, :], bank[k][:, :].rearrange("p (t c) -> p t c", t=CT), ACT.Copy,
                        scale=scales[:, SCALE_V:SCALE_V + 1],
                    ).then_inc(v_hi_ready, 1)

            def high_qk(b, n, s):
                act.wait_ge(qk_evac, b * NB + n + 1)
                px = bass.ds(n * BLK, BLK)
                nc.scalar.copy(q_both[0:CQ, px], qk_f32[s][0:CQ, :])
                nc.scalar.copy(k_hi[CQ:P, px], qk_f32[s][CQ:P, :]).then_inc(qk_hi_ready, 1)

            with act.Fori(0, B) as b:
                half = b * (NB // 2)
                split_hi(b, 0, 0, half * 16 + 16)
                act.wait_ge(scale_chain, (b + 1) * CHAIN)
                act.wait_ge(o_mm, b * (2 * PH3) + 2 * VU)
                wait_alone(act, out_stored[0], b * (CT // 2 * STORES * 16) + 16)

                def exp_pair(o, p, w):
                    n = (b * 2 + o) * NP + p
                    act.wait_ge(nmax_ready, n + 1)
                    for g in range(G):
                        strip = bass.ds((p * 2 + 1) * G + g, 1)
                        nc.scalar.activation(
                            prob[o][:, strip, :], strip_bank[2 * w + 1][:, g:g + 1, :], ACT.Exp,
                            scale=scales[0:L, S_FACTOR:S_FACTOR + 1], bias=nmax[o][:, strip],
                            accum_out=esum[o][:, strip],
                        )
                    act.wait_ge(s_shifted, n + 1)
                    strips = bass.ds(p * (2 * G), G)
                    nc.scalar.activation(prob[o][:, strips, :], prob[o][:, strips, :], ACT.Exp).then_inc(e_ready, 1)

                def double_blocks(j, rows, last):
                    for d in range(BODY):
                        i = j * BODY + d
                        split_hi(b, 2 * i + 1, 1, (half + i) * 16 + 16)
                        high_v(b, i, 0)
                        high_qk(b, 2 * i, 0)
                        if not (last and d == BODY - 1):
                            split_hi(b, 2 * i + 2, 0, (half + i) * 16 + 32)
                        high_v(b, i, 1)
                        high_qk(b, 2 * i + 1, 1)
                        if rows and d < 2:
                            exp_pair(ROW, (j - 1) * 2 + d, SP - 1)

                double_blocks(0, False, False)
                with act.Fori(1, NJ - 1) as j:
                    double_blocks(j, True, False)
                double_blocks(NJ - 1, True, True)
                for p in (NP - 2, NP - 1):
                    exp_pair(ROW, p, p % SP)
                for k in range(2 * PT):
                    act.wait_ge(v_stored[k], (b + 1) * (NB // 2 * 16) + 16)
                for d in range(BODY):
                    act.wait_ge(qk_shifted[d], (b + 1) * (NJ * 3 * 16))
                wait_alone(act, x_next_seen, (b + 1) * NB + BLOCKS)
                with act.Fori(0, NS) as i:
                    for w in range(SP):
                        exp_pair(COL, i * SP + w, w)
                act.wait_ge(s_ready, (b + 1) * (2 * NP))
                for k in range(2):
                    act.dma_start(acc[k][:, :], x_acc[b, k, :, :]).then_inc(acc_loaded[k], 16)
                act.wait_ge(shift_ready, b + 1)
                nc.scalar.activation(scaled[:, :, :], shift[:, :, :], ACT.Exp).then_inc(shift_exp, 1)

                def high_parts(o, grp, u):
                    act.wait_ge(pT_ready, (b * 2 + 1 - o) * NG + grp + 1 + U)
                    nc.scalar.activation(
                        parts[o][:, bass.ds(grp * G, G), 0, :], strip_bank[4 + u][:, :, :], ACT.Copy, scale=TOP
                    ).then_inc(p_hi_ready, 1)

                def store_rows(t, c):
                    k = t % 2
                    act.wait_ge(acc_added, ((b * CT + t) * 2 + 1) * NG + c * 2 + 2 + 4)
                    px = bass.ds(c * (VS * W), VS * W)
                    nc.scalar.activation(
                        acc[k][:, px], acc[k][:, px], ACT.Identity, bias=gbv_col[:, t:t + 1]
                    ).then_inc(bias_added, 1)
                    act.wait_ge(bias_added, (b * CT + t) * STORES + c + 1)
                    act.dma_start(out_acc[b, t, :, px], acc[k][:, px]).then_inc(out_stored[k], 16)

                with act.Fori(0, NI) as i:
                    for u in range(U):
                        high_parts(COL, i * U + u, u)
                for h in range(NG):
                    high_parts(ROW, h, h % U)
                    if h % 2 and h >= 2 * AHEAD + 1:
                        store_rows(0, h // 2 - AHEAD)
                for c in range(STORES - AHEAD, STORES):
                    store_rows(0, c)
                for t in range(1, CT):
                    if t < CT - 1:
                        k = (t + 1) % 2
                        wait_alone(act, out_stored[k], (b * (CT // 2) + (t + 1) // 2) * (STORES * 16) + 16)
                        with act.Fori(0, NV) as i:
                            for u in range(VU):
                                c = i * VU + u
                                act.wait_ge(acc_added, (b * CT + t) * 2 * NG + c * 2 + 1 + 4)
                                px = bass.ds(c * (VS * W), VS * W)
                                act.dma_start(acc[k][:, px], x_acc[b, t + 1, :, px]).then_inc(acc_loaded[k], 16)
                    with act.Fori(0, NV) as i:
                        for u in range(VU):
                            store_rows(t, i * VU + u)

        @block.vector
        def _(dve):
            dve.sem_inc(x_split, BLOCKS)
            dve.sem_inc(x_next_seen, BLOCKS)
            dve.sem_inc(x_first_seen, FIRST)
            dve.sem_inc(v_ready, VTILES)
            dve.sem_inc(acc_added, 4)
            dve.sem_inc(p_ready, U)
            dve.wait_ge(hi_ready, 1)
            nc.vector.tensor_tensor(
                wqk_lo[:, :, :], wqk_raw[:, :, :], wqk_hi[:, :, :].bitcast(F32), ALU.subtract
            ).then_inc(weights_split, 1)
            dve.wait_ge(hi_ready, 2)
            nc.vector.tensor_tensor(
                wv_lo[:, :, :], wv_raw[:, :, :], wv_hi[:, :, :].bitcast(F32), ALU.subtract
            ).then_inc(weights_split, 1)
            nc.vector.tensor_scalar(gbv_col[:, :], bv_col[:, :], gamma_col[:, 0:1], None, ALU.mult).then_inc(
                const_chain, 1
            )
            for k, src in enumerate((wqk_raw[:, :, :], wv_raw[:, :, :])):
                nc.vector.tensor_reduce(
                    bound[:, k:k + 1], src, mybir.AxisListType.XY, ALU.max, apply_absolute_value=True
                ).then_inc(const_chain, 1)
            nc.vector.tensor_reduce(wmax_own[:, 2:3], bqk_col[:, :], AX_X, ALU.max, apply_absolute_value=True)
            dve.wait_ge(const_chain, 3)
            nc.vector.tensor_scalar(wmax_own[:, 0:2], bound[:, :], float(C), None, ALU.mult).then_inc(wmax_own_ready, 1)

            def see(blk, n):
                return nc.vector.tensor_reduce(
                    xmax_blk[:, bass.ds(n, 1)], blk[:, :, :], mybir.AxisListType.XY, ALU.max, apply_absolute_value=True
                )

            def see_next(n, s, sem_round):
                dve.wait_ge(x_next_loaded[s], sem_round)
                see(x_next[s], n).then_inc(x_next_seen, 1)

            def see_all():
                nc.vector.tensor_reduce(xmax_own[:, :], xmax_blk[:, :], AX_X, ALU.max).then_inc(xmax_own_ready, 1)

            def make_scales(b):
                def step(k, ins):
                    ins.then_inc(scale_chain, 1)
                    dve.wait_ge(scale_chain, b * CHAIN + k)

                dve.wait_ge(xmax_ready, b + 1)
                nc.vector.tensor_scalar(bound[:, 1:2], xmax[:, :], wmax[:, 1:2], TINY, ALU.mult, ALU.max)
                step(1, nc.vector.tensor_scalar(bound[:, 0:1], xmax[:, :], wmax[:, 0:1], wmax[:, 2:3], ALU.mult, ALU.add))
                step(2, nc.vector.tensor_scalar(bound[:, 0:1], bound[:, 0:1], TINY, None, ALU.max))
                step(3, nc.vector.tensor_scalar(
                    floor2[:, :].bitcast(I32), bound[:, :].bitcast(I32), EXPONENT, None, ALU.bitwise_and
                ))
                step(4, nc.vector.tensor_scalar(unscale[:, :], floor2[:, :], 1.0 / TOP, None, ALU.mult))
                step(5, nc.vector.reciprocal(scales_next[:, SCALE_QK:SCALE_V + 1], unscale[:, :]))
                nc.vector.tensor_scalar(
                    scales_next[:, BIAS_QK:BIAS_QK + 1], bqk_col[:, :], scales_next[:, SCALE_QK:SCALE_QK + 1], None,
                    ALU.mult,
                )
                nc.vector.tensor_scalar(
                    scales_next[:, S_FACTOR:S_FACTOR + 1], unscale[:, 0:1], unscale[:, 0:1], None, ALU.mult
                )
                nc.vector.tensor_scalar(
                    scales_next[:, O_FACTOR:O_FACTOR + 1], unscale[:, 1:2], gamma_col[:, 0:1], 1.0 / TOP,
                    ALU.mult, ALU.mult,
                ).then_inc(scale_chain, 1)

            def split_lo(b, n, s):
                dve.wait_ge(x_hi_ready, b * NB + n + 1)
                nc.vector.tensor_tensor(
                    x_lo[s][:, :, :], x_raw[s][:, :, :], x_hi[s][:, :, :].bitcast(F32), ALU.subtract
                ).then_inc(x_split, 1)

            def low_v(b, i, s):
                for j in range(PT):
                    k = s * PT + j
                    dve.wait_ge(v_hi_ready, (b * NB + 2 * i) * PT + k + 1)
                    nc.vector.scalar_tensor_tensor(
                        out=v_out[k][:, :, 1, :], in0=bank[k][:, :].rearrange("p (t c) -> p t c", t=CT),
                        scalar=scales[:, SCALE_V:SCALE_V + 1], in1=v_out[k][:, :, 0, :], op0=ALU.mult, op1=ALU.subtract,
                    ).then_inc(v_ready, 1)

            def evac_qk(b, n, s):
                dve.wait_ge(qk_mm, b * NB + n + 1 + BLOCKS)
                dve.wait_ge(qk_ready, b * NB + n + 1)
                nc.vector.tensor_scalar(
                    qk_f32[s][:, :], bank[4 + s][:, 0:BLK], scales[:, SCALE_QK:SCALE_QK + 1],
                    scales[:, BIAS_QK:BIAS_QK + 1],
                    ALU.mult, ALU.add,
                ).then_inc(qk_evac, 1)

            with dve.Fori(0, NB // FIRST) as i:
                for s in range(FIRST):
                    dve.wait_ge(x_first_loaded[s], i * 16 + 16)
                    see(x_first[s], i * FIRST + s).then_inc(x_first_seen, 1)
            dve.wait_ge(x_first_seen, NB + FIRST)
            see_all()
            dve.wait_ge(wmax_ready, 1)
            make_scales(0)

            with dve.Fori(0, B) as b:
                dve.wait_ge(acc_added, b * (2 * PH3) + 4)
                dve.wait_ge(scale_chain, (b + 1) * CHAIN - 1)
                nc.vector.tensor_copy(scales[:, :], scales_next[:, :]).then_inc(scale_chain, 1)
                dve.wait_ge(scale_chain, (b + 1) * CHAIN)
                split_lo(b, 0, 0)
                half = b * (NB // 2)

                def sum_even(o, p):
                    dve.wait_ge(e_ready, (b * 2 + o) * NP + p + 1 + SP)
                    strips = bass.ds(p * (2 * G), G)
                    nc.vector.tensor_reduce(esum[o][:, strips], prob[o][:, strips, :], AX_X, ALU.add).then_inc(
                        esum_even, 1
                    )

                def score_pair(o, p, w, summed=None):
                    n = (b * 2 + o) * NP + p
                    both, even = bass.ds(p * (2 * G), 2 * G), bass.ds(p * (2 * G), G)
                    dve.wait_ge(s_ready, n + 1)
                    nc.vector.tensor_reduce(
                        nmax[o][:, both].rearrange("p (u g) -> p u g", u=2), pair_strips[w], AX_X, ALU.max,
                        negate=True,
                    ).then_inc(nmax_raw, 1)
                    if summed is not None:
                        sum_even(o, summed)
                    dve.wait_ge(nmax_raw, n + 1)
                    nc.vector.tensor_scalar(
                        nmax[o][:, both], nmax[o][:, both], scales[0:L, S_FACTOR:S_FACTOR + 1], None, ALU.mult
                    ).then_inc(nmax_ready, 1)
                    dve.wait_ge(nmax_ready, n + 1)
                    nc.vector.scalar_tensor_tensor(
                        out=prob[o][:, even, :], in0=strip_bank[2 * w][:, :, :],
                        scalar=scales[0:L, S_FACTOR:S_FACTOR + 1],
                        in1=nmax[o][:, even].unsqueeze(2).to_broadcast([L, G, L]), op0=ALU.mult, op1=ALU.add,
                    ).then_inc(s_shifted, 1)

                def double_blocks(j, rows, last):
                    for d in range(BODY):
                        i = j * BODY + d
                        for s in range(2):
                            if not (last and d == BODY - 1 and s == 1):
                                split_lo(b, 2 * i + 1 + s, 1 - s)
                            low_v(b, i, s)
                            evac_qk(b, 2 * i + s, s)
                            see_next(2 * i + s, s, (half + i) * 16 + 16)
                        if rows and d < 2:
                            score_pair(ROW, (j - 1) * 2 + d, SP - 1, (j - 1) * 2 if d else None)
                        elif rows:
                            sum_even(ROW, (j - 1) * 2 + 1)

                double_blocks(0, False, False)
                with dve.Fori(1, NJ - 1) as j:
                    double_blocks(j, True, False)
                double_blocks(NJ - 1, True, True)
                dve.wait_ge(x_next_seen, (b + 1) * NB + BLOCKS)
                see_all()
                for p in (NP - 2, NP - 1):
                    score_pair(ROW, p, p % SP)
                for k in range(2 * PT):
                    dve.wait_ge(v_stored[k], (b + 1) * (NB // 2 * 16) + 16)
                for w in range(SP):
                    score_pair(COL, w, w, w - 2 if w > 1 else None)
                    if w < 2:
                        sum_even(ROW, NP - 2 + w)
                with dve.Fori(1, NS) as i:
                    for w in range(SP):
                        score_pair(COL, i * SP + w, w, i * SP + w - 2)
                for p in (NP - 2, NP - 1):
                    sum_even(COL, p)
                link = b * LINKS
                dve.wait_ge(stats_T, b + 1)
                row_nmax, row_esum = bank[0][0:L, 0:L], bank[1][0:L, 0:L]
                nc.vector.tensor_tensor(njoint[:, :], row_nmax, nmax[COL][:, :], ALU.min).then_inc(dve_chain, 1)
                dve.wait_ge(dve_chain, link + 1)
                nc.vector.tensor_tensor(shift[:, ROW, :], njoint[:, :], row_nmax, ALU.subtract)
                nc.vector.tensor_tensor(shift[:, COL, :], njoint[:, :], nmax[COL][:, :], ALU.subtract).then_inc(
                    shift_ready, 1
                )
                dve.wait_ge(shift_exp, b + 1)
                nc.vector.tensor_tensor(shift[:, ROW, :], scaled[:, ROW, :], row_esum, ALU.mult).then_inc(dve_chain, 1)
                nc.vector.tensor_tensor(shift[:, COL, :], scaled[:, COL, :], esum[COL][:, :], ALU.mult).then_inc(
                    dve_chain, 1
                )
                dve.wait_ge(dve_chain, link + 3)
                nc.vector.tensor_tensor(njoint[:, :], shift[:, ROW, :], shift[:, COL, :], ALU.add).then_inc(dve_chain, 1)
                dve.wait_ge(dve_chain, link + 4)
                nc.vector.reciprocal(shift[:, ROW, :], njoint[:, :]).then_inc(dve_chain, 1)
                dve.wait_ge(dve_chain, link + 5)
                nc.vector.tensor_tensor(factor_rowT[:, :], scaled[:, ROW, :], shift[:, ROW, :], ALU.mult)
                nc.vector.tensor_tensor(factor[COL][:, :], scaled[:, COL, :], shift[:, ROW, :], ALU.mult).then_inc(
                    factors_ready, 1
                )
                dve.wait_ge(factor_T, b + 1)
                nc.vector.tensor_copy(factor[ROW][:, :], bank[2][0:L, 0:L]).then_inc(factor_row_ready, 1)
                make_scales(b + 1)
                def low_parts(o, grp, u):
                    dve.wait_ge(p_hi_ready, (b * 2 + 1 - o) * NG + grp + 1)
                    strips = bass.ds(grp * G, G)
                    nc.vector.scalar_tensor_tensor(
                        out=parts[o][:, strips, 1, :], in0=strip_bank[4 + u][:, :, :], scalar=TOP,
                        in1=parts[o][:, strips, 0, :], op0=ALU.mult, op1=ALU.subtract,
                    ).then_inc(p_ready, 1)

                def add_group(t, tp, par, o, h, first):
                    if o == COL:
                        dve.wait_ge(acc_loaded[par], b * LOADED + 16 + tp * (STORES * 16))
                    else:
                        dve.wait_ge(acc_added, first + 4)
                    dve.wait_ge(o_mm, first + h + 1 + 2 * VU)
                    return acc_strips[par][o][:, bass.ds(h * G, G), :]

                def add_to_acc(t, tp, par, o):
                    first = ((b * CT + t) * 2 + (1 - o)) * NG
                    with dve.Fori(0, NV) as i:
                        for m in range(2 * VU):
                            a = add_group(t, tp, par, o, i * (2 * VU) + m, first)
                            nc.vector.scalar_tensor_tensor(
                                out=a, in0=out_bank[m % 4], scalar=scales[:, O_FACTOR:O_FACTOR + 1], in1=a,
                                op0=ALU.mult, op1=ALU.add,
                            ).then_inc(acc_added, 1)

                for o in (COL, ROW):
                    first = (b * CT * 2 + 1 - o) * NG
                    for h in range(AHEAD):
                        low_parts(o, h, h % U)
                    for h in range(NG):
                        if h + AHEAD < NG:
                            low_parts(o, h + AHEAD, (h + AHEAD) % U)
                        a = add_group(0, 0, 0, o, h, first)
                        nc.vector.scalar_tensor_tensor(
                            out=a, in0=out_bank[h % 4], scalar=scales[:, O_FACTOR:O_FACTOR + 1], in1=a,
                            op0=ALU.mult, op1=ALU.add,
                        ).then_inc(acc_added, 1)
                for o in (COL, ROW):
                    add_to_acc(1, 0, 1, o)
                with dve.Fori(1, CT // 2) as tp:
                    for par in range(2):
                        for o in (COL, ROW):
                            add_to_acc(tp * 2 + par, tp, par, o)

        @block.tensor
        def _(pe):
            pe.sem_inc(qk_mm, BLOCKS)
            pe.sem_inc(pT_ready, U)
            pe.sem_inc(o_mm, 2 * VU)
            pe.wait_ge(weights_split, 2)
            pe.wait_ge(consts_set, 3)

            def three_products(dst, stationary, moving):
                for t in range(CT):
                    (s_hi, s_lo), (m_hi, m_lo) = stationary(t), moving(t)
                    nc.tensor.matmul(dst, s_hi, m_hi, start=(t == 0), stop=False)
                    nc.tensor.matmul(dst, s_hi, m_lo, start=False, stop=False)
                    last = nc.tensor.matmul(dst, s_lo, m_hi, start=False, stop=(t == CT - 1))
                return last

            with pe.Fori(0, B) as b:
                wait_alone(pe, acc_added, b * (2 * PH3) + 4)

                def score_pair(o, p, w):
                    strips = bass.ds(p * (2 * G), 2 * G)
                    q, k_h, k_l = q_strips[o][:, strips, :], k_hi_strips[o][:, strips, :], k_lo_strips[o][:, strips, :]
                    for u in range(2):
                        dst = strip_bank[2 * w + u]
                        for g in range(G):
                            strip = u * G + g
                            nc.tensor.matmul(
                                dst[:, g, :], q[:, strip, :], k_h[:, strip, :], start=(o == ROW or g == 0), stop=False
                            )
                            last = nc.tensor.matmul(
                                dst[:, g, :], q[:, strip, :], k_l[:, strip, :], start=False, stop=(o == ROW)
                            )
                        if o == COL:
                            last = nc.tensor.matmul(dst, ident_bf[:, :], diag_bf[:, :, :], start=False, stop=True)
                    last.then_inc(s_ready, 1)

                def double_blocks(j, rows):
                    for d in range(BODY):
                        i = j * BODY + d
                        for s in range(2):
                            n = b * NB + 2 * i + s
                            pe.wait_ge(x_split, n + 1 + BLOCKS)
                            for m in range(PT):
                                k = s * PT + m
                                px = slice(m * P, (m + 1) * P)
                                pe.wait_ge(v_ready, (b * NB + 2 * i) * PT + k + 1)
                                three_products(
                                    bank[k][:, :],
                                    lambda t: (x_hi[s][:, t, px], x_lo[s][:, t, px]),
                                    lambda t: (wv_hi[:, t, :], wv_lo[:, t, :]),
                                ).then_inc(v_mm, 1)
                            pe.wait_ge(qk_ready, n + 1)
                            three_products(
                                bank[4 + s][:, 0:BLK],
                                lambda t: (wqk_hi[:, t, :], wqk_lo[:, t, :]),
                                lambda t: (x_hi[s][:, t, :], x_lo[s][:, t, :]),
                            ).then_inc(qk_mm, 1)
                        if rows and d < 2:
                            p = (j - 1) * 2 + d
                            for e in range(BODY):
                                pe.wait_ge(qk_shifted[e], (b * NJ + j) * (3 * 16))
                            pe.wait_ge(e_ready, b * 2 * NP + p + SP)
                            score_pair(ROW, p, SP - 1)

                double_blocks(0, False)
                with pe.Fori(1, NJ) as j:
                    double_blocks(j, True)
                for d in range(BODY - 1):
                    pe.wait_ge(qk_shifted[d], (b + 1) * (NJ * 3 * 16))
                pe.wait_ge(qk_ready, (b + 1) * NB + BLOCKS)
                score_pair(ROW, NP - 2, (NP - 2) % SP)
                pe.wait_ge(qk_shifted[BODY - 1], (b + 1) * (NJ * 3 * 16))
                pe.wait_ge(e_ready, b * 2 * NP + (NP - 3) + 1 + SP)
                score_pair(ROW, NP - 1, (NP - 1) % SP)
                wait_alone(pe, v_ready, (b + 1) * (NB * PT) + VTILES)
                with pe.Fori(0, NS) as i:
                    for w in range(SP):
                        pe.wait_ge(e_ready, (b * 2 + COL) * NP + i * SP + w + 1)
                        score_pair(COL, i * SP + w, w)
                pe.wait_ge(e_ready, (b + 1) * (2 * NP) + SP)
                pe.wait_ge(esum_even, (b + 1) * (2 * NP))
                nc.tensor.transpose(bank[0][0:L, 0:L], nmax[ROW][:, :], ident[:, :])
                nc.tensor.transpose(bank[1][0:L, 0:L], esum[ROW][:, :], ident[:, :]).then_inc(stats_T, 1)
                pe.wait_ge(factors_ready, b + 1)
                nc.tensor.transpose(bank[2][0:L, 0:L], factor_rowT[:, :], ident[:, :]).then_inc(factor_T, 1)
                def transpose_group(n, u):
                    pe.wait_ge(e_grp_ready, n + 1)
                    pe.wait_ge(p_ready, n + 1)
                    for g in range(G):
                        last = nc.tensor.transpose(strip_bank[4 + u][:, g, :], e_grp[u][:, g, :], ident[:, :])
                    last.then_inc(pT_ready, 1)

                def attend(t, o, normalise=False):
                    n3 = ((b * CT + t) * 2 + (1 - o)) * NV
                    grp = (b * 2 + 1 - o) * NG
                    if normalise:
                        for h in range(AHEAD):
                            transpose_group(grp + h, h % U)
                    for load in range(NV * VU):
                        i, u = divmod(load, VU)
                        for half in range(2):
                            h = load * 2 + half
                            if normalise:
                                if h + AHEAD < NG:
                                    transpose_group(grp + h + AHEAD, (h + AHEAD) % U)
                                pe.wait_ge(p_ready, grp + h + 1 + U)
                            if half == 0:
                                pe.wait_ge(v_loaded[u], (n3 + i) * 16 + 16)
                            pe.wait_ge(acc_added, n3 * (2 * VU) + h + 1)
                            dst = out_bank[h % 4]
                            for g in range(G):
                                for a in range(2):
                                    v = v_in[u][:, half * G + g, a, :]
                                    for c in range(2):
                                        last = nc.tensor.matmul(
                                            dst[:, g, :], v, parts[o][:, h * G + g, c, :],
                                            start=(a == 0 and c == 0), stop=(a == 1 and c == 1),
                                        )
                            last.then_inc(o_mm, 1)

                pe.wait_ge(factor_row_ready, b + 1)
                for o in (COL, ROW):
                    attend(0, o, normalise=True)
                with pe.Fori(1, CT) as t:
                    for o in (COL, ROW):
                        attend(t, o)


def kernel(x, L0_conv_Wq, L0_conv_bq, L0_conv_Wk, L0_conv_bk, L0_conv_Wv, L0_conv_bv, L0_conv_gamma):
    import numpy as np
    import concourse.bacc as bacc
    from concourse.bass_utils import run_bass_kernel_spmd

    arrays = {
        "x": np.ascontiguousarray(x),
        "wqkT": np.ascontiguousarray(np.concatenate([np.asarray(L0_conv_Wq), np.asarray(L0_conv_Wk)], axis=0).T),
        "wvT": np.ascontiguousarray(np.asarray(L0_conv_Wv).T),
        "bqk": np.concatenate([np.asarray(L0_conv_bq), np.asarray(L0_conv_bk)]),
        "bv": np.ascontiguousarray(L0_conv_bv),
        "gamma": np.ascontiguousarray(L0_conv_gamma),
    }
    nc = bacc.Bacc("TRN2", target_bir_lowering=False, num_devices=1)
    args = [
        nc.dram_tensor(n, a.shape, mybir.dt.from_np(a.dtype), kind="ExternalInput").ap() for n, a in arrays.items()
    ]
    out = nc.dram_tensor("out", arrays["x"].shape, F32, kind="ExternalOutput").ap()
    criss_cross_attention(nc, *args, out)
    return run_bass_kernel_spmd(nc, [arrays], core_ids=[0]).results[0]["out"]
```
